# Optimizing a Trainium2 kernel written in Bass

```python
import numpy as np
import jax
import jax.numpy as jnp

def _softmax(x, axis=-1):
    return jax.nn.softmax(x, axis=axis)

def _gelu(x):
    return jax.nn.gelu(x, approximate=True)

def _silu(x):
    return jax.nn.silu(x)

def _sigmoid(x):
    return jax.nn.sigmoid(x)

def _layernorm(x, axis=-1, eps=1e-05):
    m = jnp.mean(x, axis=axis, keepdims=True)
    v = jnp.var(x, axis=axis, keepdims=True)
    return (x - m) / jnp.sqrt(v + eps)

def _scatter_add(tgt, idx, src, axis=0):
    return tgt.at[idx].add(src)

def _segment_sum(src, seg, n):
    return jax.ops.segment_sum(src, seg, n)
kernel_name = 'mk_gnn_ffn_d4_gnn_r16_f6a6ba'

def setup_inputs(seed: int=0):
    np.random.seed(seed)
    _w = jnp.asarray

    def _rec_inputs():
        import jax
        import jax.numpy as jnp
        _gk = jax.random.key(seed)
        x = -0.0003713 + 1 * jax.random.normal(jax.random.fold_in(_gk, 1), (3125, 256), jnp.float32)
        src = jax.random.randint(jax.random.fold_in(_gk, 2), (50000,), 0, 3125, jnp.int32)
        dst = jax.random.randint(jax.random.fold_in(_gk, 3), (50000,), 0, 3125, jnp.int32)
        _o = jnp.argsort(dst, stable=True)
        src = src[_o]
        dst = dst[_o]
        edge_weight = -7.32377e-05 + 0.176746 * jax.random.normal(jax.random.fold_in(_gk, 13), (50000,), jnp.float32)
        return (x, src, dst, edge_weight)
    x, src, dst, edge_weight = _rec_inputs()

    def _L0_gnn_setup():
        import jax, jax.numpy as jnp
        import numpy as np
        N_NODES = 3125
        NNZ = 100000
        D_FEAT = 256
        key = jax.random.key(seed)
        k_x, k_v, k_r, k_c = jax.random.split(key, 4)
        x = jax.random.normal(k_x, (N_NODES, D_FEAT), dtype=jnp.float32)
        std = 1.0 / np.sqrt(NNZ / N_NODES)
        values = jax.random.normal(k_v, (NNZ,), dtype=jnp.float32) * std
        row = jax.random.randint(k_r, (NNZ,), 0, N_NODES, dtype=jnp.int64)
        col = jax.random.randint(k_c, (NNZ,), 0, N_NODES, dtype=jnp.int64)
        return {'x': x, 'values': values, 'row': row, 'col': col}
    _L0_gnn_all = _L0_gnn_setup()
    _L0_gnn_in = {k: v for k, v in _L0_gnn_all.items() if k in ()}
    del _L0_gnn_all

    def _L0_ffn_setup():
        import jax, jax.numpy as jnp
        import numpy as np
        D_MODEL = 256
        EXPERT_DIM = 512
        NUM_EXPERTS = 8
        TOP_K = 2
        SEQ_LEN = 128
        BATCH = 2
        key = jax.random.key(seed)
        ks = jax.random.split(key, 8)
        s = 0.02
        x = jax.random.normal(ks[0], (SEQ_LEN, BATCH, D_MODEL), dtype=jnp.float32)
        Wg = jax.random.normal(ks[1], (D_MODEL, NUM_EXPERTS), dtype=jnp.float32) * s
        bg = jax.random.normal(ks[2], (NUM_EXPERTS,), dtype=jnp.float32) * s
        bias = jnp.zeros((NUM_EXPERTS,), dtype=jnp.float32)
        W1 = jax.random.normal(ks[3], (NUM_EXPERTS, D_MODEL, EXPERT_DIM), dtype=jnp.float32) * s
        b1 = jax.random.normal(ks[4], (NUM_EXPERTS, EXPERT_DIM), dtype=jnp.float32) * s
        W2 = jax.random.normal(ks[5], (NUM_EXPERTS, EXPERT_DIM, D_MODEL), dtype=jnp.float32) * s
        b2 = jax.random.normal(ks[6], (NUM_EXPERTS, D_MODEL), dtype=jnp.float32) * s
        return {'x': x, 'Wg': Wg, 'bg': bg, 'bias': bias, 'W1': W1, 'b1': b1, 'W2': W2, 'b2': b2}
    _L0_ffn_all = _L0_ffn_setup()
    _L0_ffn_in = {k: v for k, v in _L0_ffn_all.items() if k in ('Wg', 'bg', 'bias', 'W1', 'b1', 'W2', 'b2')}
    del _L0_ffn_all

    def _L1_gnn_setup():
        import jax, jax.numpy as jnp
        import numpy as np
        N, E = (3125, 50000)
        H, C_IN, C_HID, C_OUT = (4, 256, 64, 64)
        NEG_SLOPE = 0.2

        def leaky_relu(x, s=NEG_SLOPE):
            return jnp.where(x >= 0, x, s * x)

        def gat_conv(x, src, dst, W, att_src, att_dst, bias, n_nodes):
            Hh, Cc = (att_src.shape[1], att_src.shape[2])
            h = (x @ W).reshape(n_nodes, Hh, Cc)
            a_src = (h * att_src).sum(-1)
            a_dst = (h * att_dst).sum(-1)
            alpha = leaky_relu(a_src[src] + a_dst[dst])
            m = jax.ops.segment_max(alpha, dst, num_segments=n_nodes)
            e = jnp.exp(alpha - m[dst])
            denom = jax.ops.segment_sum(e, dst, num_segments=n_nodes)
            w = e / jnp.clip(denom, 1e-16)[dst]
            out = jax.ops.segment_sum(w[:, :, None] * h[src], dst, num_segments=n_nodes)
            return out.reshape(n_nodes, Hh * Cc) + bias
        key = jax.random.key(seed)
        ks = jax.random.split(key, 10)
        glorot = lambda k, shp: jax.random.normal(k, shp, jnp.float32) * np.sqrt(2.0 / (shp[0] + shp[-1]))
        return {'x': jax.random.normal(ks[0], (N, C_IN), jnp.float32), 'edge_index': jax.random.randint(ks[1], (2, E), 0, N, jnp.int32), 'W1': glorot(ks[2], (C_IN, H * C_HID)), 'att_src1': glorot(ks[3], (1, H, C_HID)), 'att_dst1': glorot(ks[4], (1, H, C_HID)), 'b1': jnp.zeros((H * C_HID,), jnp.float32), 'W2': glorot(ks[5], (H * C_HID, H * C_OUT)), 'att_src2': glorot(ks[6], (1, H, C_OUT)), 'att_dst2': glorot(ks[7], (1, H, C_OUT)), 'b2': jnp.zeros((H * C_OUT,), jnp.float32)}
    _L1_gnn_all = _L1_gnn_setup()
    _L1_gnn_in = {k: v for k, v in _L1_gnn_all.items() if k in ('W1', 'att_src1', 'att_dst1', 'b1', 'W2', 'att_src2', 'att_dst2', 'b2')}
    del _L1_gnn_all

    def _L1_ffn_setup():
        import jax, jax.numpy as jnp
        import numpy as np
        NUM_EXPERTS = 8
        TOP_K = 2
        B, S, D = (8, 512, 256)

        def _moe(tokens, router_w, w1, b1, w2, b2):
            N = tokens.shape[0]
            E = router_w.shape[0]
            logits = tokens.astype(jnp.float32) @ router_w.astype(jnp.float32).T
            probs = jax.nn.softmax(logits, axis=-1)
            rw, re = jax.lax.top_k(probs, TOP_K)
            if TOP_K > 1:
                rw = rw / jnp.maximum(rw.sum(-1, keepdims=True), 1e-12)
            rw = rw.astype(tokens.dtype)
            combine = jnp.zeros((N, E), tokens.dtype).at[jnp.arange(N)[:, None], re].set(rw)
            out = tokens
            for e in range(E):
                h = jax.nn.gelu(tokens @ w1[e] + b1[e], approximate=False)
                y = h @ w2[e] + b2[e]
                out = out + combine[:, e:e + 1] * y
            return out
        key = jax.random.key(seed)
        ks = jax.random.split(key, 4)
        scale = 1.0 / np.sqrt(D).astype(np.float32)
        return {'input_embeddings': jax.random.normal(ks[0], (B, S, D), jnp.float32), 'router_w': jax.random.normal(ks[1], (NUM_EXPERTS, D), jnp.float32) * scale, 'w1': jax.random.normal(ks[2], (NUM_EXPERTS, D, D), jnp.float32) * scale, 'b1': jnp.zeros((NUM_EXPERTS, D), jnp.float32), 'w2': jax.random.normal(ks[3], (NUM_EXPERTS, D, D), jnp.float32) * scale, 'b2': jnp.zeros((NUM_EXPERTS, D), jnp.float32)}
    _L1_ffn_all = _L1_ffn_setup()
    _L1_ffn_in = {k: v for k, v in _L1_ffn_all.items() if k in ('router_w', 'w1', 'b1', 'w2', 'b2')}
    del _L1_ffn_all

    def _L2_gnn_setup():
        import jax, jax.numpy as jnp
        import numpy as np
        N_NODES = 6250
        N_EDGES = 100000
        D = 256
        key = jax.random.key(seed)
        ks = jax.random.split(key, 8)
        h6_all = jax.random.normal(ks[0], (N_NODES, D), dtype=jnp.float32)
        edge_index = jax.random.randint(ks[1], (2, N_EDGES), 0, N_NODES, dtype=jnp.int64)
        edge_weight = jax.random.uniform(ks[2], (N_EDGES,), dtype=jnp.float32)
        s = 1.0 / np.sqrt(D)
        W = jax.random.normal(ks[3], (D, D), dtype=jnp.float32) * s
        b = jnp.zeros((D,), dtype=jnp.float32)
        W1 = jax.random.normal(ks[4], (D, D), dtype=jnp.float32) * s
        b1 = jnp.zeros((D,), dtype=jnp.float32)
        W2 = jax.random.normal(ks[5], (D, D), dtype=jnp.float32) * s
        b2 = jnp.zeros((D,), dtype=jnp.float32)
        return {'h6_all': h6_all, 'edge_index': edge_index, 'edge_weight': edge_weight, 'W': W, 'b': b, 'W1': W1, 'b1': b1, 'W2': W2, 'b2': b2}
    _L2_gnn_all = _L2_gnn_setup()
    _L2_gnn_in = {k: v for k, v in _L2_gnn_all.items() if k in ('W', 'b', 'W1', 'b1', 'W2', 'b2')}
    del _L2_gnn_all

    def _L2_ffn_setup():
        import jax, jax.numpy as jnp
        import numpy as np
        B, N, D = (16, 256, 256)
        NUM_EXPERTS, TOP_K, HEADS = (4, 2, 4)
        N_EDGES = 65536
        LN_EPS = 1e-05

        def _layernorm(x, g, b):
            mu = x.mean(-1, keepdims=True)
            var = ((x - mu) ** 2).mean(-1, keepdims=True)
            return (x - mu) * jax.lax.rsqrt(var + LN_EPS) * g + b

        def _forward(x, edge_index, W_gat, att_src, att_dst, b_gat, ln_gamma, ln_beta, W1, b1, W2, b2):
            Bc, Nc, Dc = x.shape
            M = Bc * Nc
            x_flat = x.reshape(M, Dc)
            h = (x_flat @ W_gat).reshape(M, HEADS, NUM_EXPERTS)
            loops = jnp.arange(M, dtype=edge_index.dtype)
            src = jnp.concatenate([edge_index[0], loops])
            dst = jnp.concatenate([edge_index[1], loops])
            a_src = (h * att_src).sum(-1)
            a_dst = (h * att_dst).sum(-1)
            e = jax.nn.leaky_relu(a_src[src] + a_dst[dst], negative_slope=0.2)
            e_max = jax.ops.segment_max(e, dst, num_segments=M)
            ee = jnp.exp(e - e_max[dst])
            denom = jax.ops.segment_sum(ee, dst, num_segments=M)
            alpha = ee / (denom[dst] + 1e-16)
            msg = h[src] * alpha[:, :, None]
            agg = jax.ops.segment_sum(msg, dst, num_segments=M).reshape(M, HEADS * NUM_EXPERTS) + b_gat
            scores = _layernorm(agg, ln_gamma, ln_beta).reshape(M, HEADS, NUM_EXPERTS).mean(1)
            scores = scores.reshape(Bc, Nc, NUM_EXPERTS)
            topk_s, topk_i = jax.lax.top_k(scores, TOP_K)
            w = jax.nn.softmax(topk_s, axis=-1)
            out = jnp.zeros_like(x)
            for ei in range(NUM_EXPERTS):
                g = jnp.where(topk_i == ei, w, 0.0).sum(-1)
                hh = jax.nn.gelu(x @ W1[ei] + b1[ei], approximate=False)
                out = out + g[..., None] * (hh @ W2[ei] + b2[ei])
            return out
        key = jax.random.key(seed)
        ks = jax.random.split(key, 8)
        s = 0.05
        return {'x': jax.random.normal(ks[0], (B, N, D), jnp.float32), 'W_gat': jax.random.normal(ks[1], (D, HEADS * NUM_EXPERTS), jnp.float32) * s, 'att_src': jax.random.normal(ks[2], (HEADS, NUM_EXPERTS), jnp.float32) * s, 'att_dst': jax.random.normal(ks[3], (HEADS, NUM_EXPERTS), jnp.float32) * s, 'b_gat': jnp.zeros((HEADS * NUM_EXPERTS,), jnp.float32), 'ln_gamma': jnp.ones((HEADS * NUM_EXPERTS,), jnp.float32), 'ln_beta': jnp.zeros((HEADS * NUM_EXPERTS,), jnp.float32), 'W1': jax.random.normal(ks[4], (NUM_EXPERTS, D, 2 * D), jnp.float32) * s, 'b1': jnp.zeros((NUM_EXPERTS, 2 * D), jnp.float32), 'W2': jax.random.normal(ks[5], (NUM_EXPERTS, 2 * D, D), jnp.float32) * s, 'b2': jnp.zeros((NUM_EXPERTS, D), jnp.float32), 'edge_index': jax.random.randint(ks[6], (2, N_EDGES), 0, B * N, jnp.int32)}
    _L2_ffn_all = _L2_ffn_setup()
    _L2_ffn_in = {k: v for k, v in _L2_ffn_all.items() if k in ('W_gat', 'att_src', 'att_dst', 'b_gat', 'ln_gamma', 'ln_beta', 'W1', 'b1', 'W2', 'b2', 'edge_index')}
    del _L2_ffn_all

    def _L3_gnn_setup():
        import jax, jax.numpy as jnp
        import numpy as np
        N_NODES = 3125

        def _sage_conv(x, src, dst, W_l, b_l, W_r):
            gathered = jnp.take(x, src, axis=0)
            summed = jax.ops.segment_sum(gathered, dst, num_segments=N_NODES)
            deg = jax.ops.segment_sum(jnp.ones_like(dst, dtype=x.dtype), dst, num_segments=N_NODES)
            mean_nb = summed / jnp.maximum(deg, 1.0)[:, None]
            return mean_nb @ W_l + b_l + x @ W_r
        key = jax.random.key(seed)
        ks = jax.random.split(key, 8)
        d = 256
        E = 50000
        s = 1.0 / np.sqrt(d)
        x = jax.random.normal(ks[0], (N_NODES, d), dtype=jnp.float32)
        ei = jax.random.randint(ks[1], (2, E), 0, N_NODES, dtype=jnp.int64)
        W1_l = jax.random.normal(ks[2], (d, d), dtype=jnp.float32) * s
        b1 = jnp.zeros((d,), dtype=jnp.float32)
        W1_r = jax.random.normal(ks[3], (d, d), dtype=jnp.float32) * s
        W2_l = jax.random.normal(ks[4], (d, d), dtype=jnp.float32) * s
        b2 = jnp.zeros((d,), dtype=jnp.float32)
        W2_r = jax.random.normal(ks[5], (d, d), dtype=jnp.float32) * s
        return {'x': x, 'ei': ei, 'W1_l': W1_l, 'b1': b1, 'W1_r': W1_r, 'W2_l': W2_l, 'b2': b2, 'W2_r': W2_r}
    _L3_gnn_all = _L3_gnn_setup()
    _L3_gnn_in = {k: v for k, v in _L3_gnn_all.items() if k in ('W1_l', 'b1', 'W1_r', 'W2_l', 'b2', 'W2_r')}
    del _L3_gnn_all

    def _L3_ffn_setup():
        import jax, jax.numpy as jnp
        import numpy as np
        TOP_K = 2
        key = jax.random.key(seed)
        ks = jax.random.split(key, 4)
        B, L, D, H, E = (8, 256, 256, 1024, 8)
        s = 0.02
        return {'x': jax.random.normal(ks[0], (B, L, D), jnp.float32), 'Wg': jax.random.normal(ks[1], (D, E), jnp.float32) * s, 'bg': jnp.zeros((E,), jnp.float32), 'W1': jax.random.normal(ks[2], (E, D, H), jnp.float32) * s, 'b1': jnp.zeros((E, H), jnp.float32), 'W2': jax.random.normal(ks[3], (E, H, D), jnp.float32) * s, 'b2': jnp.zeros((E, D), jnp.float32)}
    _L3_ffn_all = _L3_ffn_setup()
    _L3_ffn_in = {k: v for k, v in _L3_ffn_all.items() if k in ('Wg', 'bg', 'W1', 'b1', 'W2', 'b2')}
    del _L3_ffn_all
    return {'x': x, 'src': src, 'dst': dst, 'edge_weight': edge_weight, 'L0_ffn_Wg': _L0_ffn_in['Wg'], 'L0_ffn_bg': _L0_ffn_in['bg'], 'L0_ffn_bias': _L0_ffn_in['bias'], 'L0_ffn_W1': _L0_ffn_in['W1'], 'L0_ffn_b1': _L0_ffn_in['b1'], 'L0_ffn_W2': _L0_ffn_in['W2'], 'L0_ffn_b2': _L0_ffn_in['b2'], 'L1_gnn_W1': _L1_gnn_in['W1'], 'L1_gnn_att_src1': _L1_gnn_in['att_src1'], 'L1_gnn_att_dst1': _L1_gnn_in['att_dst1'], 'L1_gnn_b1': _L1_gnn_in['b1'], 'L1_gnn_W2': _L1_gnn_in['W2'], 'L1_gnn_att_src2': _L1_gnn_in['att_src2'], 'L1_gnn_att_dst2': _L1_gnn_in['att_dst2'], 'L1_gnn_b2': _L1_gnn_in['b2'], 'L1_ffn_router_w': _L1_ffn_in['router_w'], 'L1_ffn_w1': _L1_ffn_in['w1'], 'L1_ffn_b1': _L1_ffn_in['b1'], 'L1_ffn_w2': _L1_ffn_in['w2'], 'L1_ffn_b2': _L1_ffn_in['b2'], 'L2_gnn_W': _L2_gnn_in['W'], 'L2_gnn_b': _L2_gnn_in['b'], 'L2_gnn_W1': _L2_gnn_in['W1'], 'L2_gnn_b1': _L2_gnn_in['b1'], 'L2_gnn_W2': _L2_gnn_in['W2'], 'L2_gnn_b2': _L2_gnn_in['b2'], 'L2_ffn_W_gat': _L2_ffn_in['W_gat'], 'L2_ffn_att_src': _L2_ffn_in['att_src'], 'L2_ffn_att_dst': _L2_ffn_in['att_dst'], 'L2_ffn_b_gat': _L2_ffn_in['b_gat'], 'L2_ffn_ln_gamma': _L2_ffn_in['ln_gamma'], 'L2_ffn_ln_beta': _L2_ffn_in['ln_beta'], 'L2_ffn_W1': _L2_ffn_in['W1'], 'L2_ffn_b1': _L2_ffn_in['b1'], 'L2_ffn_W2': _L2_ffn_in['W2'], 'L2_ffn_b2': _L2_ffn_in['b2'], 'L2_ffn_edge_index': _L2_ffn_in['edge_index'], 'L3_gnn_W1_l': _L3_gnn_in['W1_l'], 'L3_gnn_b1': _L3_gnn_in['b1'], 'L3_gnn_W1_r': _L3_gnn_in['W1_r'], 'L3_gnn_W2_l': _L3_gnn_in['W2_l'], 'L3_gnn_b2': _L3_gnn_in['b2'], 'L3_gnn_W2_r': _L3_gnn_in['W2_r'], 'L3_ffn_Wg': _L3_ffn_in['Wg'], 'L3_ffn_bg': _L3_ffn_in['bg'], 'L3_ffn_W1': _L3_ffn_in['W1'], 'L3_ffn_b1': _L3_ffn_in['b1'], 'L3_ffn_W2': _L3_ffn_in['W2'], 'L3_ffn_b2': _L3_ffn_in['b2']}

def reference(x, src, dst, edge_weight, L0_ffn_Wg, L0_ffn_bg, L0_ffn_bias, L0_ffn_W1, L0_ffn_b1, L0_ffn_W2, L0_ffn_b2, L1_gnn_W1, L1_gnn_att_src1, L1_gnn_att_dst1, L1_gnn_b1, L1_gnn_W2, L1_gnn_att_src2, L1_gnn_att_dst2, L1_gnn_b2, L1_ffn_router_w, L1_ffn_w1, L1_ffn_b1, L1_ffn_w2, L1_ffn_b2, L2_gnn_W, L2_gnn_b, L2_gnn_W1, L2_gnn_b1, L2_gnn_W2, L2_gnn_b2, L2_ffn_W_gat, L2_ffn_att_src, L2_ffn_att_dst, L2_ffn_b_gat, L2_ffn_ln_gamma, L2_ffn_ln_beta, L2_ffn_W1, L2_ffn_b1, L2_ffn_W2, L2_ffn_b2, L2_ffn_edge_index, L3_gnn_W1_l, L3_gnn_b1, L3_gnn_W1_r, L3_gnn_W2_l, L3_gnn_b2, L3_gnn_W2_r, L3_ffn_Wg, L3_ffn_bg, L3_ffn_W1, L3_ffn_b1, L3_ffn_W2, L3_ffn_b2):
    import jax
    import jax.numpy as jnp

    def _L0_gnn_ref(x, values, row, col):
        import jax, jax.numpy as jnp
        import numpy as np
        N_NODES = 3125
        NNZ = 100000
        D_FEAT = 256
        msgs = values[:, None] * x[col]
        out = jax.ops.segment_sum(msgs, row, num_segments=N_NODES)
        return out

    def _L0_ffn_ref(x, Wg, bg, bias, W1, b1, W2, b2):
        import jax, jax.numpy as jnp
        import numpy as np
        D_MODEL = 256
        EXPERT_DIM = 512
        NUM_EXPERTS = 8
        TOP_K = 2
        SEQ_LEN = 128
        BATCH = 2
        x_flat = x.reshape(-1, D_MODEL)
        gate_logits = x_flat @ Wg + bg + bias
        topk_vals, topk_idx = jax.lax.top_k(gate_logits, TOP_K)
        topk_w = jax.nn.softmax(topk_vals, axis=-1)
        combine = (jax.nn.one_hot(topk_idx, NUM_EXPERTS, dtype=x.dtype) * topk_w[..., None]).sum(axis=1)
        h = jax.nn.relu(jnp.einsum('td,edh->teh', x_flat, W1) + b1)
        y = jnp.einsum('teh,ehd->ted', h, W2) + b2
        out = jnp.einsum('ted,te->td', y, combine)
        return out.reshape(x.shape)

    def _L1_gnn_ref(x, edge_index, W1, att_src1, att_dst1, b1, W2, att_src2, att_dst2, b2):
        import jax, jax.numpy as jnp
        import numpy as np
        N, E = (3125, 50000)
        H, C_IN, C_HID, C_OUT = (4, 256, 64, 64)
        NEG_SLOPE = 0.2

        def leaky_relu(x, s=NEG_SLOPE):
            return jnp.where(x >= 0, x, s * x)

        def gat_conv(x, src, dst, W, att_src, att_dst, bias, n_nodes):
            Hh, Cc = (att_src.shape[1], att_src.shape[2])
            h = (x @ W).reshape(n_nodes, Hh, Cc)
            a_src = (h * att_src).sum(-1)
            a_dst = (h * att_dst).sum(-1)
            alpha = leaky_relu(a_src[src] + a_dst[dst])
            m = jax.ops.segment_max(alpha, dst, num_segments=n_nodes)
            e = jnp.exp(alpha - m[dst])
            denom = jax.ops.segment_sum(e, dst, num_segments=n_nodes)
            w = e / jnp.clip(denom, 1e-16)[dst]
            out = jax.ops.segment_sum(w[:, :, None] * h[src], dst, num_segments=n_nodes)
            return out.reshape(n_nodes, Hh * Cc) + bias
        n = x.shape[0]
        loops = jnp.arange(n, dtype=edge_index.dtype)
        src = jnp.concatenate([edge_index[0], loops])
        dst = jnp.concatenate([edge_index[1], loops])
        h1 = gat_conv(x, src, dst, W1, att_src1, att_dst1, b1, n)
        h1 = jax.nn.relu(h1)
        out = gat_conv(h1, src, dst, W2, att_src2, att_dst2, b2, n)
        return out

    def _L1_ffn_ref(input_embeddings, router_w, w1, b1, w2, b2):
        import jax, jax.numpy as jnp
        import numpy as np
        NUM_EXPERTS = 8
        TOP_K = 2
        B, S, D = (8, 512, 256)

        def _moe(tokens, router_w, w1, b1, w2, b2):
            N = tokens.shape[0]
            E = router_w.shape[0]
            logits = tokens.astype(jnp.float32) @ router_w.astype(jnp.float32).T
            probs = jax.nn.softmax(logits, axis=-1)
            rw, re = jax.lax.top_k(probs, TOP_K)
            if TOP_K > 1:
                rw = rw / jnp.maximum(rw.sum(-1, keepdims=True), 1e-12)
            rw = rw.astype(tokens.dtype)
            combine = jnp.zeros((N, E), tokens.dtype).at[jnp.arange(N)[:, None], re].set(rw)
            out = tokens
            for e in range(E):
                h = jax.nn.gelu(tokens @ w1[e] + b1[e], approximate=False)
                y = h @ w2[e] + b2[e]
                out = out + combine[:, e:e + 1] * y
            return out
        b, s, d = input_embeddings.shape
        tokens = input_embeddings.reshape(b * s, d)
        return _moe(tokens, router_w, w1, b1, w2, b2).reshape(b, s, d)

    def _L2_gnn_ref(h6_all, edge_index, edge_weight, W, b, W1, b1, W2, b2):
        import jax, jax.numpy as jnp
        import numpy as np
        N_NODES = 6250
        N_EDGES = 100000
        D = 256
        'GCNConv(256->256, weighted, self-loops, symmetric norm) + 2-layer MLP head.'
        N = h6_all.shape[0]
        row, col = (edge_index[0], edge_index[1])
        sl = jnp.arange(N, dtype=edge_index.dtype)
        row_sl = jnp.concatenate([row, sl])
        col_sl = jnp.concatenate([col, sl])
        ew_sl = jnp.concatenate([edge_weight, jnp.ones((N,), dtype=edge_weight.dtype)])
        deg = jax.ops.segment_sum(ew_sl, row_sl, num_segments=N)
        dinv = jnp.where(deg > 0, jax.lax.rsqrt(deg), 0.0)
        norm = dinv[row_sl] * ew_sl * dinv[col_sl]
        xw = h6_all @ W
        msgs = xw[col_sl] * norm[:, None]
        h7 = jax.ops.segment_sum(msgs, row_sl, num_segments=N) + b
        h = jax.nn.relu(h7 @ W1 + b1)
        out = h @ W2 + b2
        return out

    def _L2_ffn_ref(x, W_gat, att_src, att_dst, b_gat, ln_gamma, ln_beta, W1, b1, W2, b2, edge_index):
        import jax, jax.numpy as jnp
        import numpy as np
        B, N, D = (16, 256, 256)
        NUM_EXPERTS, TOP_K, HEADS = (4, 2, 4)
        N_EDGES = 65536
        LN_EPS = 1e-05

        def _layernorm(x, g, b):
            mu = x.mean(-1, keepdims=True)
            var = ((x - mu) ** 2).mean(-1, keepdims=True)
            return (x - mu) * jax.lax.rsqrt(var + LN_EPS) * g + b

        def _forward(x, edge_index, W_gat, att_src, att_dst, b_gat, ln_gamma, ln_beta, W1, b1, W2, b2):
            Bc, Nc, Dc = x.shape
            M = Bc * Nc
            x_flat = x.reshape(M, Dc)
            h = (x_flat @ W_gat).reshape(M, HEADS, NUM_EXPERTS)
            loops = jnp.arange(M, dtype=edge_index.dtype)
            src = jnp.concatenate([edge_index[0], loops])
            dst = jnp.concatenate([edge_index[1], loops])
            a_src = (h * att_src).sum(-1)
            a_dst = (h * att_dst).sum(-1)
            e = jax.nn.leaky_relu(a_src[src] + a_dst[dst], negative_slope=0.2)
            e_max = jax.ops.segment_max(e, dst, num_segments=M)
            ee = jnp.exp(e - e_max[dst])
            denom = jax.ops.segment_sum(ee, dst, num_segments=M)
            alpha = ee / (denom[dst] + 1e-16)
            msg = h[src] * alpha[:, :, None]
            agg = jax.ops.segment_sum(msg, dst, num_segments=M).reshape(M, HEADS * NUM_EXPERTS) + b_gat
            scores = _layernorm(agg, ln_gamma, ln_beta).reshape(M, HEADS, NUM_EXPERTS).mean(1)
            scores = scores.reshape(Bc, Nc, NUM_EXPERTS)
            topk_s, topk_i = jax.lax.top_k(scores, TOP_K)
            w = jax.nn.softmax(topk_s, axis=-1)
            out = jnp.zeros_like(x)
            for ei in range(NUM_EXPERTS):
                g = jnp.where(topk_i == ei, w, 0.0).sum(-1)
                hh = jax.nn.gelu(x @ W1[ei] + b1[ei], approximate=False)
                out = out + g[..., None] * (hh @ W2[ei] + b2[ei])
            return out
        return _forward(x, edge_index, W_gat, att_src, att_dst, b_gat, ln_gamma, ln_beta, W1, b1, W2, b2)

    def _L3_gnn_ref(x, ei, W1_l, b1, W1_r, W2_l, b2, W2_r):
        import jax, jax.numpy as jnp
        import numpy as np
        N_NODES = 3125

        def _sage_conv(x, src, dst, W_l, b_l, W_r):
            gathered = jnp.take(x, src, axis=0)
            summed = jax.ops.segment_sum(gathered, dst, num_segments=N_NODES)
            deg = jax.ops.segment_sum(jnp.ones_like(dst, dtype=x.dtype), dst, num_segments=N_NODES)
            mean_nb = summed / jnp.maximum(deg, 1.0)[:, None]
            return mean_nb @ W_l + b_l + x @ W_r
        src, dst = (ei[0], ei[1])
        h = jax.nn.relu(_sage_conv(x, src, dst, W1_l, b1, W1_r))
        h = _sage_conv(h, src, dst, W2_l, b2, W2_r)
        return h

    def _L3_ffn_ref(x, Wg, bg, W1, b1, W2, b2):
        import jax, jax.numpy as jnp
        import numpy as np
        TOP_K = 2
        B, L, D = x.shape
        E = W1.shape[0]
        xf = x.reshape(-1, D)
        gate_logits = xf @ Wg + bg
        top_w, top_i = jax.lax.top_k(gate_logits, TOP_K)
        top_w = jax.nn.softmax(top_w, axis=-1)
        w_dense = jnp.sum(jax.nn.one_hot(top_i, E, dtype=xf.dtype) * top_w[..., None], axis=1)
        out = jnp.zeros_like(xf)
        for e in range(E):
            h = jax.nn.gelu(xf @ W1[e] + b1[e], approximate=False)
            out = out + w_dense[:, e:e + 1] * (h @ W2[e] + b2[e])
        return out.reshape(B, L, D)
    edge_index = jnp.stack([src, dst])
    x = x + _L0_gnn_ref(_layernorm(x, axis=-1), edge_weight, src, dst)
    x = x + _L0_ffn_ref(_layernorm(x, axis=-1)[None], L0_ffn_Wg, L0_ffn_bg, L0_ffn_bias, L0_ffn_W1, L0_ffn_b1, L0_ffn_W2, L0_ffn_b2)[0]
    x = x + _L1_gnn_ref(_layernorm(x, axis=-1), edge_index, L1_gnn_W1, L1_gnn_att_src1, L1_gnn_att_dst1, L1_gnn_b1, L1_gnn_W2, L1_gnn_att_src2, L1_gnn_att_dst2, L1_gnn_b2)
    x = x + _L1_ffn_ref(_layernorm(x, axis=-1)[None], L1_ffn_router_w, L1_ffn_w1, L1_ffn_b1, L1_ffn_w2, L1_ffn_b2)[0]
    x = x + _L2_gnn_ref(_layernorm(x, axis=-1), edge_index, edge_weight, L2_gnn_W, L2_gnn_b, L2_gnn_W1, L2_gnn_b1, L2_gnn_W2, L2_gnn_b2)
    x = x + _L2_ffn_ref(_layernorm(x, axis=-1)[None], L2_ffn_W_gat, L2_ffn_att_src, L2_ffn_att_dst, L2_ffn_b_gat, L2_ffn_ln_gamma, L2_ffn_ln_beta, L2_ffn_W1, L2_ffn_b1, L2_ffn_W2, L2_ffn_b2, L2_ffn_edge_index)[0]
    x = x + _L3_gnn_ref(_layernorm(x, axis=-1), edge_index, L3_gnn_W1_l, L3_gnn_b1, L3_gnn_W1_r, L3_gnn_W2_l, L3_gnn_b2, L3_gnn_W2_r)
    x = x + _L3_ffn_ref(_layernorm(x, axis=-1)[None], L3_ffn_Wg, L3_ffn_bg, L3_ffn_W1, L3_ffn_b1, L3_ffn_W2, L3_ffn_b2)[0]
    return x

_drawn_inputs = setup_inputs


def setup_inputs(seed=0):
    import zlib

    import numpy as np

    out = dict(_drawn_inputs(seed))
    spreads = {'L0_ffn_bias': (0.0, 0.1),
     'L1_gnn_b1': (0.0, 0.1),
     'L1_gnn_b2': (0.0, 0.1),
     'L1_ffn_b1': (0.0, 0.399),
     'L1_ffn_b2': (0.0, 0.1),
     'L2_gnn_b': (0.0, 0.8),
     'L2_gnn_b1': (0.0, 0.8),
     'L2_gnn_b2': (0.0, 0.8),
     'L2_ffn_b_gat': (0.0, 0.481),
     'L2_ffn_ln_gamma': (1.0, 0.6),
     'L2_ffn_ln_beta': (0.0, 0.8),
     'L2_ffn_b1': (0.0, 0.8),
     'L2_ffn_b2': (0.0, 0.8),
     'L3_gnn_b1': (0.0, 0.8),
     'L3_gnn_b2': (0.0, 0.8),
     'L3_ffn_bg': (0.0, 0.8),
     'L3_ffn_b1': (0.0, 0.8),
     'L3_ffn_b2': (0.0, 0.8)}
    factors = {'L0_ffn_bg': 5.892,
     'L0_ffn_b1': 8.0,
     'L0_ffn_b2': 3.91,
     'L1_gnn_att_dst1': 4.029,
     'L1_gnn_att_src2': 3.538,
     'L1_gnn_att_dst2': 8.0,
     'L2_ffn_att_src': 8.0,
     'L2_ffn_att_dst': 8.0,
     'L3_ffn_Wg': 7.576,
     'L3_ffn_W1': 8.0,
     'L3_ffn_W2': 8.0}
    for name, (base, spread) in spreads.items():
        noise = np.random.default_rng([zlib.crc32(name.encode()), seed]).standard_normal(out[name].shape)
        drawn = base * np.exp(spread * noise) if base else spread * noise
        out[name] = jnp.asarray(drawn.astype(out[name].dtype))
    for name, factor in factors.items():
        out[name] = (out[name] * factor).astype(out[name].dtype)
    return out
```

```python
import concourse.bass as bass
from concourse import mybir
from contextlib import ExitStack

F32 = mybir.dt.float32
I32 = mybir.dt.int32
U32 = mybir.dt.uint32
ALU = mybir.AluOpType
ACT = mybir.ActivationFunctionType
AX = mybir.AxisListType.X
DVE = mybir.EngineType.DVE
PE = mybir.EngineType.PE
RMAX = bass.bass_isa.ReduceOp.max

P = 128
N = 3125
D = 256
KD = D // P
NT = -(-N // P)
NPAD = NT * P
LAST = N - (NT - 1) * P
TG = 5
NG = NT // TG
HEADS = 4
LN_EPS = 1e-5
SLOPE = 0.2
EG = 4
GB = 4
AHEAD = GB - 1
U = EG * GB
CHUNK = 400
NCH = NPAD // CHUNK
GUARD = 60.0
SC = 8


class Edges:

    def __init__(self, name, count, parts, drops):
        self.name, self.parts, self.cols = name, parts, count // parts
        self.tiles = -(-(count // P + NT) // U) * U
        self.slots = P * self.tiles
        self.rows = self.slots + (count if drops else 0)
        self.drops = drops


def program(nc, a, out):
    LA = Edges("by_src", 50000, 125, False)
    LB = Edges("by_dst", 50000, 125, False)
    LF = Edges("by_ffn_dst", 65536, 128, True)
    TMAX = LF.tiles
    whole = ExitStack()
    with whole:
        scopes = [0]
        spent = []

        def scope(ctx):
            scopes[0] += 1
            n = scopes[0]
            if len(spent) > 80:
                nc.clear_and_free_semaphores(list(spent))
                nc.all_engine_barrier()
                spent.clear()

            def sb(name, shape, dt=F32):
                return ctx.enter_context(nc.sbuf_tensor(f"{name}_{n}", shape, dt))

            def pb(name, shape, dt=F32):
                return ctx.enter_context(nc.psum_tensor(f"{name}_{n}", shape, dt))

            def sem(name):
                s = nc.alloc_semaphore(f"{name}_{n}")
                ctx.callback(spent.append, s)
                return s
            return sb, pb, sem

        sb, _, sem = scope(whole)
        passed = sem("passed")

        def hold(eng, sem, value):
            eng.wait_ge(sem, value)
            eng.sem_inc(passed, 1)

        def linker(eng, sem, base=0):
            at = [0]

            def link(ins):
                at[0] += 1
                ins.then_inc(sem, 1)
                if isinstance(base, int):
                    eng.wait_ge(sem, base + at[0])
                else:
                    hold(eng, sem, base + at[0])
            return link

        X = sb("X", [P, NT, D])
        ident = sb("ident", [P, P])
        iota_row = sb("iota_row", [P, P])
        before = sb("before", [P, P])
        ones = sb("ones", [P, P])
        eps = sb("eps", [P, 1])
        DINV = sb("DINV", [P, NT])
        list_dram = {e.name: nc.dram_tensor(f"list_{e.name}", [e.rows, 4], F32, kind="Internal").ap()
                     for e in (LA, LB, LF)}
        blk = {e.name: sb(f"blk_{e.name}", [1, e.tiles + 3 * EG], I32) for e in (LA, LB, LF)}
        W1TAB = D + 1
        WGAT = D + HEADS
        WF = 16 + HEADS
        tab1 = [nc.dram_tensor(f"table_ones{i}", [NPAD, W1TAB], F32, kind="Internal").ap() for i in range(3)]
        tabg = [nc.dram_tensor(f"table_gat{i}", [NPAD, WGAT], F32, kind="Internal").ap() for i in range(2)]
        tabx = nc.dram_tensor("table_gcn", [NPAD, D], F32, kind="Internal").ap()
        tabf = nc.dram_tensor("table_ffn_gat", [NPAD, WF], F32, kind="Internal").ap()

        sort_ctx, sort_ffn_ctx = ExitStack(), ExitStack()
        rec, adr = {}, {}
        for c_, lists in ((sort_ffn_ctx, (LF,)), (sort_ctx, (LA, LB))):
            sbs, _, _ = scope(c_)
            for e in lists:
                rec[e.name] = sbs(f"rec_{e.name}", [P, e.cols, 4])
                adr[e.name] = sbs(f"adr_{e.name}", [P, e.cols], I32)

        def setup():
            with ExitStack() as ctx:
                sb, pb, sem = scope(ctx)
                C = LF.cols
                key = {e.name: sb(f"key_{e.name}", [P, e.cols], I32) for e in (LA, LB, LF)}
                gid = sb("gid_ffn", [P, LF.cols], I32)
                ewt = sb("ewt", [P, LA.cols])
                onec = sb("onec", [P, C])
                iot = sb("iot", [P, TMAX])
                ioti = sb("ioti", [P, TMAX], I32)
                eidi = sb("eidi", [P, C], I32)
                eid = sb("eid", [P, C])
                mask = sb("mask", [P, C])
                scan = sb("scan", [P, C])
                part = sb("part", [P, C])
                blkf = sb("blkf", [P, C])
                rank = sb("rank", [P, C])
                ti = sb("ti", [P, C], I32)
                tj = sb("tj", [P, C], I32)
                tot = sb("tot", [P, NT])
                ni = sb("ni", [P, NT], I32)
                nj = sb("nj", [P, NT], I32)
                nf = sb("nf", [P, NT])
                tend = sb("tend", [P, NT])
                off = sb("off", [P, NT])
                tb = sb("tb", [P, TMAX])
                nullrec = sb("nullrec", [P, TMAX, 4])
                sti = sb("sti", [P, 2, SC], I32)
                stage = sb("stage", [P, 2, SC, 4])
                pre = pb("pre", [P, NT])
                cnt = pb("cnt", [P, NT])
                loaded, made, nulls, totals = sem("loaded"), sem("made"), sem("nulls"), sem("totals")
                prefixed, chain, placed = sem("prefixed"), sem("chain"), sem("placed")
                staged, null_ready, own = sem("staged"), sem("null_ready"), sem("own")
                landed = [sem(f"landed{q}") for q in range(2)]

                with nc.Block() as block:
                    @block.sync
                    def _(sp):
                        def load(e, src, dst):
                            sp.dma_start(dst[0:e.parts, :], src.rearrange("(p c) -> p c", c=e.cols)).then_inc(loaded, 16)
                        load(LA, a["src"], key[LA.name])
                        load(LB, a["dst"], key[LB.name])
                        load(LA, a["edge_weight"], ewt)
                        load(LF, a["L2_ffn_edge_index"][0, :], gid)
                        load(LF, a["L2_ffn_edge_index"][1, :], key[LF.name])
                        sp.dma_start(X[:, 0:NT - 1, :], a["x"][0:(NT - 1) * P, :].rearrange("(t p) d -> p t d", p=P)).then_inc(loaded, 16)
                        sp.wait_ge(null_ready, 3)
                        sp.dma_start(X[0:LAST, NT - 1, :], a["x"][(NT - 1) * P:N, :]).then_inc(loaded, 16)
                        for e in (LA, LB, LF):
                            sp.dma_start(list_dram[e.name][0:e.slots, :].rearrange("(p t) r -> p t r", p=P),
                                         nullrec[:, 0:e.tiles, :]).then_inc(nulls, 16)
                        sp.wait_ge(nulls, 48)
                        sp.wait_ge(loaded, 7 * 16)

                    @block.gpsimd
                    def _(pool):
                        nc.gpsimd.memset(X[:, NT - 1, :], 0.0).then_inc(null_ready, 1)
                        nc.gpsimd.memset(nullrec[:, :, :], 0.0).then_inc(null_ready, 1)
                        nc.gpsimd.memset(ones[:, :], 1.0).then_inc(own, 1)
                        nc.gpsimd.memset(ident[:, :], 0.0).then_inc(own, 1)
                        pool.wait_ge(null_ready, 2)
                        nc.gpsimd.memset(nullrec[:, :, 1:2], -1.0).then_inc(null_ready, 1)
                        nc.gpsimd.iota(ioti[:, :], pattern=[[1, TMAX]], base=0, channel_multiplier=0).then_inc(made, 1)
                        nc.gpsimd.iota(eidi[:, :], pattern=[[1, C]], base=LF.slots, channel_multiplier=C).then_inc(made, 1)
                        pool.wait_ge(own, 2)
                        nc.gpsimd.affine_select(out=ident[:, :], in_=ident[:, :], compare_op=ALU.not_equal, fill=1.0,
                                                base=0, pattern=[[-1, P]], channel_multiplier=1).then_inc(made, 1)
                        nc.gpsimd.affine_select(out=before[:, :], in_=ones[:, :], compare_op=ALU.is_gt, fill=0.0,
                                                base=0, pattern=[[1, P]], channel_multiplier=-1).then_inc(made, 1)
                        nc.gpsimd.memset(eps[:, :], LN_EPS).then_inc(made, 1)
                        pool.wait_ge(nulls, 48)
                        pool.wait_ge(placed, 1)
                        scatter(pool, LA, sti, stage, staged, landed)

                    @block.vector
                    def _(dve):
                        link = linker(dve, chain)
                        dve.wait_ge(made, 5)
                        nc.vector.memset(onec[:, :], 1.0)
                        link(nc.vector.tensor_copy(iot[:, :], ioti[:, :]))
                        link(nc.vector.tensor_copy(iota_row[:, :], ioti[:, 0:P]))
                        link(nc.vector.tensor_copy(eid[:, :], eidi[:, :]))
                        dve.wait_ge(loaded, 7 * 16)
                        loops = 0
                        for n, e in enumerate((LA, LB, LF)):
                            q, c = e.parts, e.cols
                            k, r = key[e.name], rec[e.name]
                            v = [z[0:q, 0:c] for z in (mask, scan, part, blkf, rank, ti, tj, onec)]
                            m_, s_, p_, b_, r_, ti_, tj_, one_ = v
                            link(nc.vector.tensor_scalar(ti_, k[0:q, :], 7, None, ALU.logical_shift_right))
                            link(nc.vector.tensor_copy(b_, ti_))
                            link(nc.vector.tensor_scalar(tj_, k[0:q, :], P - 1, None, ALU.bitwise_and))
                            link(nc.vector.tensor_copy(r[0:q, :, 1], tj_))
                            if e is LA:
                                link(nc.vector.tensor_copy(r[0:q, :, 0], key[LB.name][0:q, :]))
                                link(nc.vector.tensor_copy(r[0:q, :, 2], ewt[0:q, :]))
                            elif e is LB:
                                link(nc.vector.tensor_copy(r[0:q, :, 0], key[LA.name][0:q, :]))
                                link(nc.vector.memset(r[0:q, :, 2], 1.0))
                            else:
                                link(nc.vector.tensor_scalar(r[0:q, :, 0], gid[0:q, :], float(N - 1), 0.0, ALU.min, ALU.max))
                                link(nc.vector.memset(r[0:q, :, 2], 1.0))
                            link(nc.vector.memset(r[0:q, :, 3], 0.0))
                            link(nc.vector.memset(r_, 0.0))
                            PER = 5
                            with dve.Fori(0, NT) as b:
                                at = [0]

                                def inner(ins, base=b * PER, at=at, n=n):
                                    at[0] += 1
                                    ins.then_inc(ranks[n], 1)
                                    dve.wait_ge(ranks[n], base + at[0])
                                bcol = iot[0:q, bass.ds(b, 1)]
                                inner(nc.vector.tensor_scalar(m_, b_, bcol, None, ALU.is_equal))
                                inner(nc.vector.tensor_tensor_scan(s_, one_, m_, 0.0, ALU.mult, ALU.add))
                                inner(nc.vector.tensor_copy(tot[0:q, bass.ds(b, 1)], s_[:, c - 1:c]))
                                inner(nc.vector.tensor_tensor(p_, m_, s_, ALU.mult))
                                inner(nc.vector.tensor_tensor(r_, r_, p_, ALU.add))
                            nc.vector.memset(tb[0:1, :], 0.0).then_inc(totals, 1)
                            dve.wait_ge(totals, n + 1)
                            dve.wait_ge(prefixed, n + 1)
                            link(nc.vector.tensor_scalar(ni[:, :], cnt[:, :], float(P - 1), None, ALU.add))
                            link(nc.vector.tensor_scalar(nj[:, :], ni[:, :], 7, None, ALU.logical_shift_right))
                            link(nc.vector.tensor_copy(nf[:, :], nj[:, :]))
                            link(nc.vector.tensor_tensor_scan(tend[:, :], onec[:, 0:NT], nf[:, :], 0.0, ALU.mult, ALU.add))
                            link(nc.vector.tensor_tensor(nf[:, :], tend[:, :], nf[:, :], ALU.subtract))
                            link(nc.vector.scalar_tensor_tensor(out=off[:, :], in0=nf[:, :], scalar=float(P), in1=pre[:, :],
                                                                op0=ALU.mult, op1=ALU.add))
                            with dve.Fori(0, NT) as b:
                                at2 = [0]

                                def inner2(ins, base=b * 3, at=at2, n=n):
                                    at[0] += 1
                                    ins.then_inc(bases[n], 1)
                                    dve.wait_ge(bases[n], base + at[0])
                                inner2(nc.vector.tensor_scalar(p_, b_, iot[0:q, bass.ds(b, 1)], off[0:q, bass.ds(b, 1)],
                                                               ALU.is_equal, ALU.mult))
                                inner2(nc.vector.tensor_tensor(r_, r_, p_, ALU.add))
                                inner2(nc.vector.scalar_tensor_tensor(out=tb[0:1, 0:e.tiles], in0=iot[0:1, 0:e.tiles],
                                                                      scalar=tend[0:1, bass.ds(b, 1)], in1=tb[0:1, 0:e.tiles],
                                                                      op0=ALU.is_ge, op1=ALU.add))
                            link(nc.vector.memset(blk[e.name][0:1, :], 0))
                            link(nc.vector.tensor_scalar(blk[e.name][0:1, EG:EG + e.tiles], tb[0:1, 0:e.tiles], float(NT - 1), None, ALU.min))
                            link(nc.vector.tensor_scalar(ti_, r_, 1.0, None, ALU.subtract))
                            link(nc.vector.tensor_scalar(tj_, ti_, P - 1, None, ALU.bitwise_and))
                            link(nc.vector.tensor_scalar(ti_, ti_, 7, None, ALU.arith_shift_right))
                            link(nc.vector.scalar_tensor_tensor(out=p_, in0=tj_, scalar=float(e.tiles), in1=ti_,
                                                                op0=ALU.mult, op1=ALU.add))
                            if e.drops:
                                link(nc.vector.tensor_scalar(m_, b_, float(NT), None, ALU.is_ge))
                                link(nc.vector.tensor_tensor(s_, eid[0:q, :], p_, ALU.subtract))
                                link(nc.vector.tensor_tensor(s_, s_, m_, ALU.mult))
                                link(nc.vector.tensor_tensor(p_, p_, s_, ALU.add))
                            nc.vector.tensor_copy(adr[e.name][0:q, :], p_).then_inc(placed, 1)
                            dve.wait_ge(placed, n + 1)

                    @block.tensor
                    def _(pe):
                        pe.wait_ge(made, 5)
                        for n, e in enumerate((LA, LB, LF)):
                            pe.wait_ge(totals, n + 1)
                            nc.tensor.matmul(pre[:, :], before[0:e.parts, :], tot[0:e.parts, :], start=True, stop=True)
                            nc.tensor.matmul(cnt[:, :], ones[0:e.parts, :], tot[0:e.parts, :], start=True, stop=True).then_inc(prefixed, 1)

        def scatter(pool, e, sti, stage, staged, landed):
            q, per = e.parts, 16 * SC
            trips = e.cols // (2 * SC) - 1

            def turn(h, first, n):
                nc.gpsimd.tensor_copy(stage[0:q, h, :, :], rec[e.name][0:q, bass.ds(first, SC), :]).then_inc(staged, 1)
                nc.gpsimd.tensor_copy(sti[0:q, h, :], adr[e.name][0:q, bass.ds(first, SC)]).then_inc(staged, 1)
                hold(pool, staged, n * 2 + 2)
                for c in range(SC):
                    pool.indirect_dma_start(list_dram[e.name], bass.IndirectOffsetOnAxis(sti[0:q, h, c:c + 1], 0),
                                            stage[0:q, h, c, :], None).then_inc(landed[h], 16)

            turn(0, 0, 0)
            with pool.Fori(0, trips) as i:
                turn(1, i * (2 * SC) + SC, i * 2 + 1)
                pool.wait_ge(landed[0], i * per + per)
                turn(0, i * (2 * SC) + 2 * SC, i * 2 + 2)
                pool.wait_ge(landed[1], i * per + per)
            turn(1, e.cols - SC, 2 * trips + 1)
            for h in range(2):
                pool.wait_ge(landed[h], per * (trips + 1))

        with ExitStack() as rk:
            _, _, semr = scope(rk)
            ranks = [semr(f"ranks{n}") for n in range(3)]
            bases = [semr(f"bases{n}") for n in range(3)]
            setup()

        def row_broadcast(v):
            return v.partition_broadcast(P)

        def ln_stats(dve, link, waits, i, st, mv, var_ready, rstd_ready, rstd):
            for j in range(TG):
                nc.vector.bn_stats(st[:, j, :], X[:, bass.ds(i * TG + j, 1), :].rearrange("p a d -> p (a d)")).then_inc(link, 1)
            hold(dve, link, i * (2 * TG) + TG)
            for j in range(TG):
                nc.vector.bn_aggr(mv[:, j, :], st[:, j, :]).then_inc(link, 1)
            hold(dve, link, i * (2 * TG) + 2 * TG)
            nc.vector.engine_nop().then_inc(var_ready, 1)
            hold(dve, rstd_ready, i + 1)

        def prep(name, ln, src, W, nout, TB, XT=None, attS=None, attD=None, AD=None, ones_col=None,
                 table=None, logits=None, resid=False, raw=None, scale=None, c=64):
            width = HEADS
            with ExitStack() as ctx:
                sb, pb, sem = scope(ctx)
                st = sb("st", [P, TG, 6])
                mv = sb("mv", [P, TG, 2])
                sd = sb("sd", [P, TG])
                rstd = sb("rstd", [P, TG])
                xs = sb("xs", [P, TG, D])
                turned = W is not None or XT is not None
                xts = sb("xts", [P, TG, KD, P]) if turned else None
                psT = pb("psT", [P, 3, 2, D]) if turned else None
                psL = pb("psL", [P, 3, 2, D]) if W is not None else None
                if W is not None:
                    Wsb = sb("Wsb", [P, KD, nout])
                if logits is not None:
                    LG, Wg, bgs, E, wg_view = logits
                    Wgs = sb("Wgs", [P, KD, 8])
                    bgb = sb("bgb", [P, max(len(bgs), 1), E])
                    psG = pb("psG", [P, TG, 8])
                if AD is not None:
                    sbc = sb("sbc", [P, width, c])
                    dbc = sb("dbc", [P, width, c])
                    tmp = sb("tmp", [P, 2, TG, width, c])
                    amax = sb("amax", [P, 64])
                    gmax = sb("gmax", [P, HEADS])
                    zt = sb("zt", [P, NT, HEADS])
                    ut = sb("ut", [P, NT, HEADS])
                loaded, stats, var_ready, sd_ready = sem("loaded"), sem("stats"), sem("var_ready"), sem("sd_ready")
                xs_ready, turned_s, turned_c, done = sem("xs_ready"), sem("turned_s"), sem("turned_c"), sem("done")
                mult, kept, chain, stored = sem("mult"), sem("kept"), sem("chain"), sem("stored")
                xtc, att, red, whole_s, gm = sem("xtc"), sem("att"), sem("red"), sem("whole_s"), sem("gm")
                nloads = 0
                loads = []
                if W is not None:
                    loads.append((Wsb[:, :, :], W.rearrange("(k p) n -> p k n", p=P)))
                if logits is not None:
                    loads += [(Wgs[:, k, 0:E], wg_view[:, k, :]) for k in range(KD)]
                    loads += [(bgb[:, n, :], row_broadcast(v)) for n, v in enumerate(bgs)]
                if AD is not None:
                    loads.append((sbc[:, :, :].rearrange("p h c -> p (h c)"), row_broadcast(attS)))
                    loads.append((dbc[:, :, :].rearrange("p h c -> p (h c)"), row_broadcast(attD)))

                with nc.Block() as block:
                    @block.sync
                    def _(sp):
                        for dst, s_ in loads:
                            sp.dma_start(dst, s_, allow_slow_non_contiguous=True).then_inc(loaded, 16)
                        if loads:
                            sp.wait_ge(loaded, 16 * len(loads))
                        if table is not None:
                            sp.wait_ge(whole_s, 1)
                            sp.dma_start(table.rearrange("(t p) w -> p t w", p=P), (TB if raw is None else raw)[:, :, :]).then_inc(stored, 16)
                            sp.wait_ge(stored, 16)

                    @block.scalar
                    def _(act):
                        if loads:
                            act.wait_ge(loaded, 16 * len(loads))
                        with act.Fori(0, NG) as i:
                            if ln:
                                act.wait_ge(var_ready, i + 1)
                                nc.scalar.activation(sd[:, :], mv[:, :, 1], ACT.Sqrt, bias=eps[:, 0:1]).then_inc(sd_ready, 1)
                            if turned:
                                act.wait_ge(turned_s, i * TG + TG)
                                for j in range(TG):
                                    nc.scalar.copy(xts[:, j, :, :].rearrange("p k n -> p (k n)"), psT[:, j // 2, j % 2, :]).then_inc(turned_c, 1)
                            if XT is not None:
                                for j in range(TG):
                                    nc.scalar.copy(XT[:, :, bass.ds((i * TG + j) * P, P)],
                                                   psT[:, j // 2, j % 2, :].rearrange("p (k n) -> p k n", k=KD)).then_inc(xtc, 1)
                            if W is not None:
                                act.wait_ge(mult, i * TG + TG)
                                for j in range(TG):
                                    nc.scalar.activation(TB[:, bass.ds(i * TG + j, 1), 0:nout].rearrange("p a d -> p (a d)"),
                                                         psL[:, j // 2, j % 2, 0:nout], ACT.Copy,
                                                         scale=1.0 if scale is None else scale[:, bass.ds(i * TG + j, 1)]).then_inc(kept, 1)

                    @block.gpsimd
                    def _(pool):
                        if AD is not None:
                            pool.wait_ge(gm, 1)
                            nc.gpsimd.partition_all_reduce(gmax[:, :], amax[:, 0:HEADS], P, RMAX).then_inc(gm, 1)

                    @block.tensor
                    def _(pe):
                        if turned:
                            if loads:
                                pe.wait_ge(loaded, 16 * len(loads))
                            with pe.Fori(0, NG) as i:
                                pe.wait_ge(xs_ready, i + 1)
                                for j in range(TG):
                                    for k in range(KD):
                                        m = nc.tensor.transpose(psT[:, j // 2, j % 2, k * P:(k + 1) * P], xs[:, j, k * P:(k + 1) * P], ident[:, :])
                                    m.then_inc(turned_s, 1)
                                for j in range(TG):
                                    pe.wait_ge(turned_c, i * TG + j + 1)
                                    if W is not None:
                                        for k in range(KD):
                                            m = nc.tensor.matmul(psL[:, j // 2, j % 2, 0:nout], xts[:, j, k, :], Wsb[:, k, :],
                                                                 start=(k == 0), stop=(k == KD - 1))
                                        m.then_inc(mult, 1)
                                    if logits is not None:
                                        for k in range(KD):
                                            m = nc.tensor.matmul(psG[:, j, 0:E], xts[:, j, k, :], Wgs[:, k, 0:E],
                                                                 start=(k == 0), stop=(k == KD - 1))
                                        m.then_inc(att, 1)

                    @block.vector
                    def _(dve):
                        if loads:
                            dve.wait_ge(loaded, 16 * len(loads))
                        if ones_col is not None:
                            nc.vector.memset((TB if raw is None else raw)[:, :, ones_col:ones_col + 1], 1.0).then_inc(done, 1)
                        else:
                            dve.sem_inc(done, 1)
                        with dve.Fori(0, NG) as i:
                            hold(dve, done, i + 1)
                            if ln:
                                ln_stats(dve, stats, None, i, st, mv, var_ready, sd_ready, rstd)
                                nc.vector.reciprocal(rstd[:, :], sd[:, :]).then_inc(chain, 1)
                                hold(dve, chain, i + 1)
                            for j in range(TG):
                                t = bass.ds(i * TG + j, 1)
                                dst = xs[:, j, :] if turned else TB[:, t, 0:D].rearrange("p a d -> p (a d)")
                                if ln:
                                    m = nc.vector.tensor_scalar(dst, X[:, t, :].rearrange("p a d -> p (a d)"), mv[:, j, 0:1],
                                                                rstd[:, j:j + 1], ALU.subtract, ALU.mult)
                                else:
                                    m = nc.vector.tensor_copy(dst, src[:, t, 0:D].rearrange("p a d -> p (a d)"))
                            m.then_inc(xs_ready, 1)
                            if raw is not None:
                                hold(dve, xs_ready, i + 1)
                                nc.vector.tensor_copy(raw[:, bass.ds(i * TG, TG), 0:D], xs[:, :, :]).then_inc(red, 1)
                                hold(dve, red, i + 1)
                            if resid:
                                hold(dve, xs_ready, i + 1)
                                xg = X[:, bass.ds(i * TG, TG), :]
                                nc.vector.tensor_tensor(xg, xg, xs[:, :, :], ALU.add).then_inc(red, 1)
                                hold(dve, red, i + 1)
                            if logits is not None:
                                hold(dve, att, (i + 1) * TG)
                                lg = LG[:, bass.ds(i * TG, TG), 0:E]
                                nb = len(bgs)
                                for n in range(max(nb, 1)):
                                    if nb == 0:
                                        nc.vector.tensor_copy(lg, psG[:, :, 0:E]).then_inc(whole_s, 1)
                                    else:
                                        in0 = psG[:, :, 0:E] if n == 0 else lg
                                        nc.vector.tensor_tensor(lg, in0, bgb[:, n:n + 1, :].to_broadcast([P, TG, E]), ALU.add).then_inc(whole_s, 1)
                                        hold(dve, whole_s, i * nb + n + 1)
                            if XT is not None:
                                hold(dve, xtc, (i + 1) * TG)
                            if W is not None:
                                hold(dve, kept, (i + 1) * TG)
                            if AD is not None:
                                h5 = TB[:, bass.ds(i * TG, TG), 0:width * c].rearrange("p t (h c) -> p t h c", h=width)
                                nc.vector.tensor_tensor(tmp[:, 0, :, :, :], h5, sbc[:, :, :].unsqueeze(1).to_broadcast([P, TG, width, c]), ALU.mult)
                                nc.vector.tensor_tensor(tmp[:, 1, :, :, :], h5, dbc[:, :, :].unsqueeze(1).to_broadcast([P, TG, width, c]), ALU.mult).then_inc(att, 1)
                                hold(dve, att, i + 1)
                                nc.vector.tensor_reduce(TB[:, bass.ds(i * TG, TG), width * c:width * c + width], tmp[:, 0, :, :, :], AX, ALU.add)
                                nc.vector.tensor_reduce(AD[:, bass.ds(i * TG, TG), 0:width], tmp[:, 1, :, :, :], AX, ALU.add).then_inc(red, 1)
                                hold(dve, red, i + 1)
                            nc.vector.engine_nop().then_inc(done, 1)
                        if AD is not None:
                            base = NG
                            As = TB[:, :, width * c:width * c + width]
                            link = linker(dve, red, base=NG)
                            nc.vector.tensor_reduce(amax[:, 0:HEADS], As.rearrange("p t h -> p h t"), AX, ALU.max).then_inc(gm, 1)
                            dve.wait_ge(gm, 2)
                            link(nc.vector.tensor_tensor(zt[:, :, :], AD[:, :, 0:HEADS], gmax[:, :].unsqueeze(1).to_broadcast([P, NT, HEADS]), ALU.add))
                            link(nc.vector.scalar_tensor_tensor(out=ut[:, :, :], in0=zt[:, :, :], scalar=SLOPE, in1=zt[:, :, :], op0=ALU.mult, op1=ALU.max))
                            link(nc.vector.tensor_tensor(zt[:, :, :], AD[:, :, 0:HEADS], As, ALU.add))
                            link(nc.vector.scalar_tensor_tensor(out=zt[:, :, :], in0=zt[:, :, :], scalar=SLOPE, in1=zt[:, :, :], op0=ALU.mult, op1=ALU.max))
                            link(nc.vector.scalar_tensor_tensor(out=AD[:, :, HEADS:2 * HEADS], in0=zt[:, :, :], scalar=GUARD, in1=ut[:, :, :], op0=ALU.add, op1=ALU.min))
                        if table is not None:
                            dve.wait_ge(done, NG + 1)
                            nc.vector.engine_nop().then_inc(whole_s, 1)

        def edge_sum(name, e, table, W, acc, AD=None, c=64):
            with ExitStack() as ctx:
                sb, pb, sem = scope(ctx)
                R = sb("R", [P, e.tiles + AHEAD * EG, 4])
                ids = sb("ids", [P, GB, EG], I32)
                G = sb("G", [P, GB, EG, W])
                S = sb("S", [P, GB, EG, P])
                psM = pb("psM", [P, EG, 512])
                if AD is not None:
                    St = sb("St", [P, GB, EG, P])
                    z = sb("z", [P, EG, HEADS])
                    psS = pb("psS", [P, 2, 512])
                    psE = pb("psE", [P, 2, 64, 2 * HEADS])
                loaded, ids_ready, s_ready = sem("loaded"), sem("ids_ready"), sem("s_ready")
                gathered = [sem(f"gathered{g}") for g in range(GB)]
                summed, added, cleared = sem("summed"), sem("added"), sem("cleared")
                turned_s, turned_c, fetched, scored, powered, weighed = (sem("turned_s"), sem("turned_c"), sem("fetched"),
                                                                       sem("scored"), sem("powered"), sem("weighed"))
                z_step = sem("z_step")
                trips = e.tiles // U
                FREE = (GB - 1) * EG

                with nc.Block() as block:
                    @block.sync
                    def _(sp):
                        sp.dma_start(R[:, 0:e.tiles, :], list_dram[e.name][0:e.slots, :].rearrange("(p t) r -> p t r", p=P)).then_inc(loaded, 16)
                        sp.wait_ge(loaded, 16)

                    @block.scalar
                    def _(act):
                        def take_ids(i, k0):
                            if i is None:
                                act.wait_ge(summed, k0 * EG + EG)
                                src = R[:, k0 * EG:k0 * EG + EG, 0]
                            else:
                                act.wait_ge(summed, i * U + (k0 * EG + EG))
                                src = R[:, bass.ds(i * U + k0 * EG, EG), 0]
                            nc.scalar.copy(ids[:, k0 % GB, :], src).then_inc(ids_ready, 1)

                        def keep_turned(i, k0):
                            act.wait_ge(turned_s, k0 + 1 if i is None else i * GB + (k0 + 1))
                            nc.scalar.copy(St[:, k0 % GB, :, :].rearrange("p j n -> p (j n)"), psS[:, k0 % 2, :]).then_inc(turned_c, 1)

                        act.wait_ge(loaded, 16)
                        act.wait_ge(cleared, 1)
                        for k in range(AHEAD):
                            take_ids(None, k)
                        if AD is not None:
                            keep_turned(None, 0)
                            keep_turned(None, 1)
                            act.wait_ge(scored, 1)
                            nc.scalar.activation(G[:, 0, :, HEADS * c:HEADS * c + HEADS], z[:, :, :], ACT.Exp).then_inc(powered, 1)
                        with act.Fori(0, trips) as i:
                            for g in range(GB):
                                take_ids(i, g + AHEAD)
                                if AD is not None:
                                    keep_turned(i, g + 2)
                                    act.wait_ge(scored, i * GB + (g + 2))
                                    nc.scalar.activation(G[:, (g + 1) % GB, :, HEADS * c:HEADS * c + HEADS], z[:, :, :], ACT.Exp).then_inc(powered, 1)

                    @block.gpsimd
                    def _(pool):
                        def gather(g):
                            for j in range(EG):
                                pool.indirect_dma_start(G[:, g, j, :], None, table,
                                                        bass.IndirectOffsetOnAxis(ids[:, g, j:j + 1], 0)).then_inc(gathered[g], 16)

                        with pool.Fori(0, trips) as i:
                            for g in range(GB):
                                hold(pool, ids_ready, i * GB + (g + 1))
                                gather(g)
                        if AD is not None:
                            pool.wait_ge(ids_ready, trips * GB + 1)
                            gather(0)

                    @block.tensor
                    def _(pe):
                        def turn(i, k0):
                            g = k0 % GB
                            hold(pe, s_ready, k0 + 1 if i is None else i * GB + (k0 + 1))
                            for j in range(EG):
                                m = nc.tensor.transpose(psS[:, k0 % 2, j * P:(j + 1) * P], S[:, g, j, :], ident[:, :])
                            m.then_inc(turned_s, 1)

                        def fetch(i, k0, bl):
                            g = k0 % GB
                            pe.wait_ge(turned_c, k0 + 1 if i is None else i * GB + (k0 + 1))
                            for j in range(EG):
                                m = nc.tensor.matmul(psE[:, k0 % 2, j, :], St[:, g, j, :],
                                                     AD[:, bass.ds(bl[j], 1), :].rearrange("p a h -> p (a h)"), start=True, stop=True)
                            m.then_inc(fetched, 1)

                        pe.sem_inc(summed, FREE)
                        pe.wait_ge(cleared, 1)
                        for j in range(EG):
                            nc.tensor.matmul(psM[:, j, 0:W], S[:, GB - 1, j, :], G[:, GB - 1, j, :], start=True, stop=True).then_inc(summed, 1)
                        if AD is not None:
                            _, bl = nc.values_load_multi_w_load_instructions(
                                blk[e.name][0:1, EG:3 * EG], engines=[PE], min_val=0, max_val=NT - 1,
                                skip_runtime_bounds_check_because="the chip clamps the block to the last one")
                            for k in range(2):
                                turn(None, k)
                                fetch(None, k, bl[k * EG:(k + 1) * EG])
                        with pe.Fori(0, trips) as i:
                            if AD is not None:
                                _, bl = nc.values_load_multi_w_load_instructions(
                                    blk[e.name][0:1, bass.ds(i * U + 3 * EG, U)], engines=[PE], min_val=0, max_val=NT - 1,
                                    skip_runtime_bounds_check_because="the chip clamps the block to the last one")
                            for g in range(GB):
                                if AD is not None:
                                    turn(i, g + 2)
                                    pe.wait_ge(weighed, i * GB + (g + 1))
                                else:
                                    pe.wait_ge(s_ready, i * GB + (g + 1))
                                    pe.wait_ge(gathered[g], i * (16 * EG) + 16 * EG)
                                for j in range(EG):
                                    pe.wait_ge(added, i * U + (g * EG + j + 1 + EG))
                                    nc.tensor.matmul(psM[:, j, 0:W], S[:, g, j, :], G[:, g, j, :], start=True, stop=True).then_inc(summed, 1)
                                if AD is not None:
                                    fetch(i, g + 2, bl[g * EG:(g + 1) * EG])

                    @block.vector
                    def _(dve):
                        def make_s(i, k0, j):
                            t = slice(k0 * EG + j, k0 * EG + j + 1) if i is None else bass.ds(i * U + (k0 * EG + j), 1)
                            m = nc.vector.tensor_scalar(S[:, k0 % GB, j, :], iota_row[:, :], R[:, t, 1:2].rearrange("p a r -> p (a r)"),
                                                        R[:, t, 2:3].rearrange("p a r -> p (a r)"), ALU.is_equal, ALU.mult)
                            if j == EG - 1:
                                m.then_inc(s_ready, 1)

                        def add_up(i, n0, b):
                            dve.wait_ge(summed, n0 + FREE + 1 if i is None else i * U + (n0 + FREE + 1))
                            dve.wait_ge(added, n0 + EG if i is None else i * U + (n0 + EG))
                            ab = acc[:, bass.ds(b, 1), 0:W].rearrange("p a d -> p (a d)")
                            nc.vector.tensor_tensor(ab, ab, psM[:, n0 % EG, 0:W], ALU.add).then_inc(added, 1)

                        def score(i, k0):
                            g = k0 % GB
                            gas = G[:, g, :, HEADS * c:HEADS * c + HEADS]
                            dve.wait_ge(fetched, k0 + 1 if i is None else i * GB + (k0 + 1))
                            there = (k0 // GB + 1) * (16 * EG)
                            dve.wait_ge(gathered[g], there if i is None else i * (16 * EG) + there)
                            nc.vector.tensor_tensor(z[:, :, :], gas, psE[:, k0 % 2, 0:EG, 0:HEADS], ALU.add).then_inc(z_step, 1)
                            dve.wait_ge(z_step, 2 * k0 + 1 if i is None else i * (2 * GB) + (2 * k0 + 1))
                            nc.vector.scalar_tensor_tensor(out=z[:, :, :], in0=z[:, :, :], scalar=SLOPE, in1=z[:, :, :], op0=ALU.mult, op1=ALU.max).then_inc(z_step, 1)
                            dve.wait_ge(z_step, 2 * k0 + 2 if i is None else i * (2 * GB) + (2 * k0 + 2))
                            nc.vector.tensor_tensor(z[:, :, :], z[:, :, :], psE[:, k0 % 2, 0:EG, HEADS:2 * HEADS], ALU.subtract).then_inc(scored, 1)

                        nc.vector.memset(R[:, e.tiles:, 1:4], -1.0)
                        nc.vector.memset(R[:, e.tiles:, 0:1], 0.0)
                        nc.vector.memset(S[:, GB - 1, :, :], 0.0)
                        nc.vector.memset(G[:, GB - 1, :, :], 0.0).then_inc(cleared, 1)
                        dve.wait_ge(loaded, 16)
                        for k in range(AHEAD):
                            for j in range(EG):
                                make_s(None, k, j)
                        nc.vector.memset(acc[:, :, 0:W], 0.0).then_inc(added, EG)
                        if AD is not None:
                            score(None, 0)
                        with dve.Fori(0, trips) as i:
                            _, bl = nc.values_load_multi_w_load_instructions(
                                blk[e.name][0:1, bass.ds(i * U, U)], engines=[DVE], min_val=0, max_val=NT - 1,
                                skip_runtime_bounds_check_because="the chip clamps the block to the last one")
                            for g in range(GB):
                                if AD is not None:
                                    dve.wait_ge(powered, i * GB + (g + 1))
                                    gas = G[:, g, :, HEADS * c:HEADS * c + HEADS]
                                    gh = G[:, g, :, 0:HEADS * c].rearrange("p j (h c) -> p j h c", h=HEADS)
                                    nc.vector.tensor_tensor(gh, gh, gas.unsqueeze(3).to_broadcast([P, EG, HEADS, c]), ALU.mult).then_inc(weighed, 1)
                                    for j in range(EG):
                                        add_up(i, g * EG + j, bl[g * EG + j])
                                    score(i, g + 1)
                                    for j in range(EG):
                                        make_s(i, g + AHEAD, j)
                                else:
                                    for j in range(EG):
                                        add_up(i, g * EG + j, bl[g * EG + j])
                                        make_s(i, g + AHEAD, j)
                        _, bl = nc.values_load_multi_w_load_instructions(
                            blk[e.name][0:1, e.tiles:e.tiles + EG], engines=[DVE], min_val=0, max_val=NT - 1,
                            skip_runtime_bounds_check_because="the chip clamps the block to the last one")
                        for j in range(EG):
                            add_up(None, e.tiles + j, bl[j])

        def sweep(per, steps, trips=NG, waits=None):
            with ExitStack() as ctx:
                _, _, sem = scope(ctx)
                chain = sem("chain")
                with nc.Block() as block:
                    @block.vector
                    def _(dve):
                        with dve.Fori(0, trips) as i:
                            steps(linker(dve, chain, i * per), bass.ds(i * TG, TG))

        def tiles_bc(v, n):
            return v.unsqueeze(1).to_broadcast([P, TG, n])

        def bias_load(dst, v):
            with ExitStack() as ctx:
                _, _, sem = scope(ctx)
                there = sem("there")
                with nc.Block() as block:
                    @block.sync
                    def _(sp):
                        sp.dma_start(dst, row_broadcast(v)).then_inc(there, 16)
                        sp.wait_ge(there, 16)

        def attention_end(TB, AD, acc, c, bias, into):
            with ExitStack() as ctx:
                sb, _, sem = scope(ctx)
                z = sb("z", [P, NT, HEADS])
                own = sb("own", [P, NT, HEADS])
                rden = sb("rden", [P, NT, HEADS])
                bb = sb("bb", [P, HEADS * c])
                chain, scored, powered, there = sem("chain"), sem("scored"), sem("powered"), sem("there")
                done = sem("done")
                As = TB[:, :, HEADS * c:HEADS * c + HEADS]
                with nc.Block() as block:
                    @block.sync
                    def _(sp):
                        sp.dma_start(bb[:, :], row_broadcast(bias)).then_inc(there, 16)
                        sp.wait_ge(there, 16)

                    @block.scalar
                    def _(act):
                        act.wait_ge(scored, 1)
                        nc.scalar.activation(own[:, :, :], z[:, :, :], ACT.Exp).then_inc(powered, 1)

                    @block.vector
                    def _(dve):
                        link = linker(dve, chain)
                        link(nc.vector.tensor_tensor(z[:, :, :], As, AD[:, :, 0:HEADS], ALU.add))
                        link(nc.vector.scalar_tensor_tensor(out=z[:, :, :], in0=z[:, :, :], scalar=SLOPE, in1=z[:, :, :], op0=ALU.mult, op1=ALU.max))
                        nc.vector.tensor_tensor(z[:, :, :], z[:, :, :], AD[:, :, HEADS:2 * HEADS], ALU.subtract).then_inc(scored, 1)
                        dve.wait_ge(powered, 1)
                        link(nc.vector.tensor_tensor(rden[:, :, :], acc[:, :, HEADS * c:HEADS * c + HEADS], own[:, :, :], ALU.add))
                        link(nc.vector.reciprocal(rden[:, :, :], rden[:, :, :]))
                        dve.wait_ge(there, 16)
                        with dve.Fori(0, NG) as i:
                            t = bass.ds(i * TG, TG)
                            step = linker(dve, done, i * 5)
                            h4 = TB[:, t, 0:HEADS * c].rearrange("p t (h c) -> p t h c", h=HEADS)
                            a4 = acc[:, t, 0:HEADS * c].rearrange("p t (h c) -> p t h c", h=HEADS)
                            step(nc.vector.tensor_tensor(h4, h4, own[:, t, :].unsqueeze(3).to_broadcast([P, TG, HEADS, c]), ALU.mult))
                            step(nc.vector.tensor_tensor(a4, a4, h4, ALU.add))
                            step(nc.vector.tensor_tensor(a4, a4, rden[:, t, :].unsqueeze(3).to_broadcast([P, TG, HEADS, c]), ALU.mult))
                            av = acc[:, t, 0:HEADS * c]
                            step(nc.vector.tensor_tensor(av, av, tiles_bc(bb[:, :], HEADS * c), ALU.add))
                            into(step, t, av)

        def gates(LG, gT, E):
            with ExitStack() as ctx:
                sb, pb, sem = scope(ctx)
                M8 = sb("M8", [P, NT, 8])
                I8 = sb("I8", [P, NT, 8], U32)
                If = sb("If", [P, NT, 8])
                dd = sb("dd", [P, NT, 1])
                ee = sb("ee", [P, NT, 1])
                den = sb("den", [P, NT, 1])
                w2 = sb("w2", [P, NT, 1])
                ga = sb("ga", [P, NT, 8])
                gb = sb("gb", [P, NT, 8])
                ps = pb("ps", [8, 2, 4, P])
                best, found, chain, dready, eready = sem("best"), sem("found"), sem("chain"), sem("dready"), sem("eready")
                gready, turned, copied = sem("gready"), sem("turned"), sem("copied")
                quads = -(-NT // 4)
                with nc.Block() as block:
                    @block.vector
                    def _(dve):
                        link = linker(dve, chain)
                        if E < 8:
                            link(nc.vector.memset(LG[:, :, E:8], -3.0e38))
                        for t in range(NT):
                            nc.vector.max(M8[:, t, :], LG[:, t, :]).then_inc(best, 1)
                        dve.wait_ge(best, NT)
                        for t in range(NT):
                            nc.vector.max_index(I8[:, t, :], M8[:, t, :], LG[:, t, :]).then_inc(found, 1)
                        nc.vector.tensor_tensor(dd[:, :, :], M8[:, :, 1:2], M8[:, :, 0:1], ALU.subtract).then_inc(dready, 1)
                        dve.wait_ge(found, NT)
                        link(nc.vector.tensor_copy(If[:, :, :], I8[:, :, :]))
                        dve.wait_ge(eready, 1)
                        link(nc.vector.tensor_scalar(den[:, :, :], ee[:, :, :], 1.0, None, ALU.add))
                        link(nc.vector.reciprocal(den[:, :, :], den[:, :, :]))
                        link(nc.vector.tensor_tensor(w2[:, :, :], ee[:, :, :], den[:, :, :], ALU.mult))
                        io = iota_row[:, 0:8].unsqueeze(1).to_broadcast([P, NT, 8])

                        def bc(v):
                            return v.to_broadcast([P, NT, 8])
                        link(nc.vector.tensor_tensor(ga[:, :, :], io, bc(If[:, :, 0:1]), ALU.is_equal))
                        link(nc.vector.tensor_tensor(ga[:, :, :], ga[:, :, :], bc(den[:, :, :]), ALU.mult))
                        link(nc.vector.tensor_tensor(gb[:, :, :], io, bc(If[:, :, 1:2]), ALU.is_equal))
                        link(nc.vector.tensor_tensor(gb[:, :, :], gb[:, :, :], bc(w2[:, :, :]), ALU.mult))
                        nc.vector.tensor_tensor(ga[:, :, :], ga[:, :, :], gb[:, :, :], ALU.add).then_inc(gready, 1)
                        for q in range(quads):
                            n = min(4, NT - 4 * q)
                            dve.wait_ge(turned, q + 1)
                            nc.vector.tensor_copy(gT[:, 4 * q * P:(4 * q + n) * P], ps[:, q % 2, 0:n, :].rearrange("e n p -> e (n p)")).then_inc(copied, 1)

                    @block.scalar
                    def _(act):
                        act.wait_ge(dready, 1)
                        nc.scalar.activation(ee[:, :, :], dd[:, :, :], ACT.Exp).then_inc(eready, 1)

                    @block.tensor
                    def _(pe):
                        pe.wait_ge(gready, 1)
                        for q in range(quads):
                            if q >= 2:
                                pe.wait_ge(copied, q - 1)
                            for n in range(min(4, NT - 4 * q)):
                                m = nc.tensor.transpose(ps[:, q % 2, n, :], ga[:, 4 * q + n, :], ident[:, :])
                            m.then_inc(turned, 1)

        def experts(name, XT, gT, accT, E, Hd, func, w1, b1, w2, b2, beside=None):
            nh = Hd // P
            with ExitStack() as ctx:
                sb, pb, sem = scope(ctx)
                w1s = sb("w1s", [P, 2, KD, Hd])
                w2s = sb("w2s", [P, 2, nh, D])
                Ht = sb("Ht", [P, 2, nh, CHUNK])
                b1r = sb("b1r", [E * nh, P])
                b1t = sb("b1t", [P, E * nh])
                b1e = sb("b1e", [P, 2, nh])
                b2s = sb("b2s", [E, D])
                sel = sb("sel", [E, 2, P])
                gBs = sb("gBs", [P, 2, CHUNK])
                tmp = sb("tmp", [P, 2, CHUNK])
                psH = pb("psH", [P, 2, 512])
                psY = pb("psY", [P, 2, KD, 512])
                psG = pb("psG", [P, 2, 512])
                loaded = [sem(f"weights{s}") for s in range(2)]
                small, turned, b1_ready = sem("small"), sem("turned"), sem("b1_ready")
                sel_ready, hidden, activated, gated, summed = sem("sel_ready"), sem("hidden"), sem("activated"), sem("gated"), sem("summed")
                gcopied, weighed, added, started, b2_sum, bsel = sem("gcopied"), sem("weighed"), sem("added"), sem("started"), sem("b2_sum"), sem("bsel")
                w1v = w1.rearrange("e (k p) h -> e p k h", p=P)
                w2v = w2.rearrange("e (k p) d -> e p k d", p=P)
                PAIRS = NCH // 2

                with nc.Block() as block:
                    @block.sync
                    def _(sp):
                        sp.dma_start(b1r[:, :], b1.rearrange("e (h p) -> (e h) p", p=P)).then_inc(small, 16)
                        sp.dma_start(b2s[:, :], b2).then_inc(small, 16)
                        with sp.Fori(0, E // 2) as i:
                            for s in range(2):
                                sp.wait_ge(started, i * 2 + s + 1)
                                sp.dma_start(w1s[:, s, :, :], w1v[bass.ds(i * 2 + s, 1)].rearrange("a p k h -> p (a k) h")).then_inc(loaded[s], 16)
                                sp.dma_start(w2s[:, s, :, :], w2v[bass.ds(i * 2 + s, 1)].rearrange("a p k d -> p (a k) d")).then_inc(loaded[s], 16)
                        for s in range(2):
                            sp.wait_ge(loaded[s], 32 * (E // 2))
                        sp.wait_ge(small, 32)

                    if beside is not None:
                        @block.gpsimd
                        def _(pool):
                            beside(pool)

                    @block.tensor
                    def _(pe):
                        pe.wait_ge(small, 32)
                        nc.tensor.transpose(psG[:, 0, 0:E * nh], b1r[:, :], ident[0:E * nh, 0:E * nh]).then_inc(turned, 1)
                        pe.wait_ge(b1_ready, 1)
                        with pe.Fori(0, PAIRS) as j:
                            for q in range(2):
                                pe.wait_ge(bsel, j * 2 + q + 1)
                                for k in range(KD):
                                    m = nc.tensor.matmul(psY[:, q, k, 0:CHUNK], b2s[:, k * P:(k + 1) * P],
                                                         gT[0:E, bass.ds((j * 2 + q) * CHUNK, CHUNK)], start=True, stop=True)
                                m.then_inc(b2_sum, 1)
                        pe.sem_inc(started, 2)
                        with pe.Fori(0, E // 2) as i:
                            for s in range(2):
                                pe.wait_ge(loaded[s], i * 32 + 32)
                                hold(pe, sel_ready, i * 2 + s + 1)
                                with pe.Fori(0, PAIRS) as j:
                                    n0 = (i * 2 + s) * NCH + j * 2
                                    for q in range(2):
                                        col = bass.ds((j * 2 + q) * CHUNK, CHUNK)
                                        n = n0 + q
                                        pe.wait_ge(weighed, n + 1)
                                        nc.tensor.matmul(psG[:, q, 0:CHUNK], sel[:, s, :], gT[0:E, col], start=True, stop=True).then_inc(gated, 1)
                                        for h in range(nh):
                                            pe.wait_ge(activated, n * nh + h + 1)
                                            for k in range(KD):
                                                m = nc.tensor.matmul(psH[:, h % 2, 0:CHUNK], w1s[:, s, k, h * P:(h + 1) * P], XT[:, k, col],
                                                                     start=(k == 0), stop=(k == KD - 1))
                                            m.then_inc(hidden, 1)
                                        pe.wait_ge(activated, n * nh + nh + 2)
                                        for k in range(KD):
                                            for h in range(nh):
                                                m = nc.tensor.matmul(psY[:, q, k, 0:CHUNK], w2s[:, s, h, k * P:(k + 1) * P], Ht[:, q, h, :],
                                                                     start=(h == 0), stop=(h == nh - 1))
                                        m.then_inc(summed, 1)
                                pe.wait_ge(summed, (i * 2 + s) * NCH + NCH)
                                pe.sem_inc(started, 1)

                    @block.scalar
                    def _(act):
                        act.wait_ge(turned, 1)
                        nc.scalar.copy(b1t[:, :], psG[:, 0, 0:E * nh]).then_inc(b1_ready, 1)
                        act.sem_inc(activated, 2)
                        with act.Fori(0, E // 2) as i:
                            for s in range(2):
                                act.wait_ge(sel_ready, i * 2 + s + 1)
                                with act.Fori(0, PAIRS) as j:
                                    n0 = (i * 2 + s) * NCH + j * 2
                                    for q in range(2):
                                        n = n0 + q
                                        act.wait_ge(gated, n + 1)
                                        nc.scalar.copy(gBs[:, q, :], psG[:, q, 0:CHUNK]).then_inc(gcopied, 1)
                                        for h in range(nh):
                                            act.wait_ge(hidden, n * nh + h + 1)
                                            nc.scalar.activation(Ht[:, q, h, :], psH[:, h % 2, 0:CHUNK], func, bias=b1e[:, s, h:h + 1]).then_inc(activated, 1)

                    @block.vector
                    def _(dve):
                        dve.sem_inc(bsel, 2)
                        with dve.Fori(0, PAIRS) as j:
                            for q in range(2):
                                hold(dve, b2_sum, j * 2 + q + 1)
                                nc.vector.tensor_copy(accT[:, :, bass.ds((j * 2 + q) * CHUNK, CHUNK)], psY[:, q, :, 0:CHUNK]).then_inc(bsel, 1)
                        dve.wait_ge(bsel, NCH + 2)
                        dve.wait_ge(b1_ready, 1)
                        dve.sem_inc(weighed, 2)
                        nc.vector.engine_nop().then_inc(added, 1)
                        with dve.Fori(0, E // 2) as i:
                            for s in range(2):
                                nc.vector.tensor_copy(b1e[:, s, :], b1t[:, bass.ds((i * 2 + s) * nh, nh)])
                                nc.vector.tensor_copy(sel[:, s, :], ident[0:E, bass.ds(i * 2 + s, 1)].to_broadcast([E, P])).then_inc(sel_ready, 1)
                                with dve.Fori(0, PAIRS) as j:
                                    n0 = (i * 2 + s) * NCH + j * 2
                                    for q in range(2):
                                        n = n0 + q
                                        col = bass.ds((j * 2 + q) * CHUNK, CHUNK)
                                        dve.wait_ge(gcopied, n + 1)
                                        dve.wait_ge(summed, n + 1)
                                        for k in range(KD):
                                            m = nc.vector.tensor_tensor(tmp[:, k, :], psY[:, q, k, 0:CHUNK], gBs[:, q, :], ALU.mult)
                                        m.then_inc(weighed, 1)
                                        dve.wait_ge(weighed, n + 3)
                                        nc.vector.tensor_tensor(accT[:, :, col], accT[:, :, col], tmp[:, :, :], ALU.add).then_inc(added, 1)
                                        hold(dve, added, n + 2)

        def experts_end(accT, last=False):
            with ExitStack() as ctx:
                sb, pb, sem = scope(ctx)
                y = sb("y", [P, TG, KD, P])
                ps = pb("ps", [P, 3, 2, D])
                copied, turned, added, stored = sem("copied"), sem("turned"), sem("added"), sem("stored")
                with nc.Block() as block:
                    @block.scalar
                    def _(act):
                        with act.Fori(0, NG) as i:
                            act.wait_ge(added, i + 1)
                            for j in range(TG):
                                nc.scalar.copy(y[:, j, :, :], accT[:, :, bass.ds((i * TG + j) * P, P)]).then_inc(copied, 1)

                    @block.tensor
                    def _(pe):
                        with pe.Fori(0, NG) as i:
                            for j in range(TG):
                                pe.wait_ge(copied, i * TG + j + 1)
                                for k in range(KD):
                                    m = nc.tensor.transpose(ps[:, j // 2, j % 2, k * P:(k + 1) * P], y[:, j, k, :], ident[:, :])
                                m.then_inc(turned, 1)

                    @block.vector
                    def _(dve):
                        dve.sem_inc(added, 1)
                        with dve.Fori(0, NG) as i:
                            dve.wait_ge(turned, i * TG + TG)
                            for j in range(TG):
                                xv = X[:, bass.ds(i * TG + j, 1), :].rearrange("p a d -> p (a d)")
                                m = nc.vector.tensor_tensor(xv, xv, ps[:, j // 2, j % 2, :], ALU.add)
                            m.then_inc(added, 1)

                    if last:
                        @block.sync
                        def _(sp):
                            sp.wait_ge(added, NG + 1)
                            sp.dma_start(out[0:(NT - 1) * P, :].rearrange("(t p) d -> p t d", p=P), X[:, 0:NT - 1, :]).then_inc(stored, 16)
                            sp.dma_start(out[(NT - 1) * P:N, :], X[0:LAST, NT - 1, :]).then_inc(stored, 16)
                            sp.wait_ge(stored, 32)


        def add_to_x(bias_row, parts_of):
            def steps(link, t):
                for v in parts_of:
                    link(nc.vector.tensor_tensor(X[:, t, :], X[:, t, :], v[:, t, 0:D], ALU.add))
                if bias_row is not None:
                    link(nc.vector.tensor_tensor(X[:, t, :], X[:, t, :], tiles_bc(bias_row[:, :], D), ALU.add))
            sweep(len(parts_of) + (bias_row is not None), steps)

        with ExitStack() as ctx:
            sb, pb, sem = scope(ctx)
            TB = sb("TB", [P, NT, W1TAB])
            acc = sb("acc", [P, NT, W1TAB])
            prep("spmm", True, X, None, 0, TB, ones_col=D, table=tab1[0])
            edge_sum("spmm", LA, tab1[0], W1TAB, acc)
            add_to_x(None, [acc])
            with ExitStack() as c2:
                sb2, _, sem = scope(c2)
                deg, safe = sb2("deg", [P, NT]), sb2("safe", [P, NT])
                chain, safe_ready, rooted = sem("chain"), sem("safe_ready"), sem("rooted")
                with nc.Block() as block:
                    @block.vector
                    def _(dve):
                        link = linker(dve, chain)
                        link(nc.vector.tensor_scalar(deg[:, :], acc[:, :, D], 1.0, None, ALU.add))
                        nc.vector.tensor_scalar(safe[:, :], deg[:, :], 2e-35, None, ALU.max).then_inc(safe_ready, 1)
                        dve.wait_ge(rooted, 1)
                        link(nc.vector.reciprocal(safe[:, :], safe[:, :]))
                        link(nc.vector.tensor_scalar(deg[:, :], deg[:, :], 0.0, None, ALU.is_gt))
                        link(nc.vector.tensor_tensor(DINV[:, :], safe[:, :], deg[:, :], ALU.mult))

                    @block.scalar
                    def _(act):
                        act.wait_ge(safe_ready, 1)
                        nc.scalar.activation(safe[:, :], safe[:, :], ACT.Sqrt).then_inc(rooted, 1)

        def expert_layer(name, E, Hd, func, wg_view, gate_biases, w1, b1, w2, b2, resid=False, beside=None, last=False):
            with ExitStack() as ctx:
                sb, pb, sem = scope(ctx)
                XT = sb("XT", [P, KD, NPAD])
                accT = sb("accT", [P, KD, NPAD])
                gT = sb("gT", [8, NPAD])
                LG = sb("LG", [P, NT, 8])
                prep(name, True, X, None, 0, None, XT=XT, logits=(LG, None, gate_biases, E, wg_view), resid=resid)
                gates(LG, gT, E)
                experts(name, XT, gT, accT, E, Hd, func, w1, b1, w2, b2, beside)
                experts_end(accT, last)

        def scattering(ctx, e):
            sb, _, sem = scope(ctx)
            sti = sb("sti", [P, 2, SC], I32)
            stage = sb("stage", [P, 2, SC, 4])
            staged = sem("staged")
            landed = [sem(f"landed{q}") for q in range(2)]
            return lambda pool: scatter(pool, e, sti, stage, staged, landed)

        with ExitStack() as ctx:
            sort_more = scattering(ctx, LB)
            expert_layer("ffn0", 8, 512, ACT.Relu, a["L0_ffn_Wg"].rearrange("(k p) e -> p k e", p=P),
                         [a["L0_ffn_bg"], a["L0_ffn_bias"]], a["L0_ffn_W1"], a["L0_ffn_b1"], a["L0_ffn_W2"], a["L0_ffn_b2"],
                         beside=sort_more)
        sort_ctx.close()

        with ExitStack() as ctx:
            sb, pb, sem = scope(ctx)
            TB = sb("TB", [P, NT, WGAT])
            acc = sb("acc", [P, NT, WGAT])
            AD = sb("AD", [P, NT, 2 * HEADS])

            def relu_into(step, t, v):
                step(nc.vector.tensor_scalar(v, v, 0.0, None, ALU.max))

            def x_into(step, t, v):
                step(nc.vector.tensor_tensor(X[:, t, :], X[:, t, :], v, ALU.add))
            for n, into in ((1, relu_into), (2, x_into)):
                prep(f"gat{n}", n == 1, X if n == 1 else acc, a[f"L1_gnn_W{n}"], D, TB,
                     attS=a[f"L1_gnn_att_src{n}"].rearrange("a h c -> (a h c)"),
                     attD=a[f"L1_gnn_att_dst{n}"].rearrange("a h c -> (a h c)"), AD=AD, table=tabg[n - 1])
                edge_sum(f"gat{n}", LB, tabg[n - 1], WGAT, acc, AD=AD, c=64)
                attention_end(TB, AD, acc, 64, a[f"L1_gnn_b{n}"], into)

        with ExitStack() as ctx:
            sort_more = scattering(ctx, LF)
            expert_layer("ffn1", 8, 256, ACT.Gelu, a["L1_ffn_router_w"].rearrange("e (k p) -> p k e", p=P), [],
                         a["L1_ffn_w1"], a["L1_ffn_b1"], a["L1_ffn_w2"], a["L1_ffn_b2"], resid=True, beside=sort_more)
        sort_ffn_ctx.close()

        with ExitStack() as ctx:
            sb, pb, sem = scope(ctx)
            TB = sb("TB", [P, NT, D])
            acc = sb("acc", [P, NT, D])
            bb = sb("bb", [P, D])
            prep("gcn", True, X, a["L2_gnn_W"], D, TB, scale=DINV, table=tabx)
            edge_sum("gcn", LA, tabx, D, acc)
            bias_load(bb[:, :], a["L2_gnn_b"])

            def normed(link, t):
                av = acc[:, t, :]
                link(nc.vector.tensor_tensor(av, av, TB[:, t, :], ALU.add))
                link(nc.vector.tensor_tensor(av, av, DINV[:, t].unsqueeze(2).to_broadcast([P, TG, D]), ALU.mult))
                link(nc.vector.tensor_tensor(av, av, tiles_bc(bb[:, :], D), ALU.add))
            sweep(3, normed)
            prep("gcn_w1", False, acc, a["L2_gnn_W1"], D, TB)
            bias_load(bb[:, :], a["L2_gnn_b1"])

            def hidden(link, t):
                link(nc.vector.tensor_tensor(TB[:, t, :], TB[:, t, :], tiles_bc(bb[:, :], D), ALU.add))
                link(nc.vector.tensor_scalar(TB[:, t, :], TB[:, t, :], 0.0, None, ALU.max))
            sweep(2, hidden)
            prep("gcn_w2", False, TB, a["L2_gnn_W2"], D, acc)
            bias_load(bb[:, :], a["L2_gnn_b2"])
            add_to_x(bb, [acc])

        with ExitStack() as ctx:
            sb, pb, sem = scope(ctx)
            XT = sb("XT", [P, KD, NPAD])
            accT = sb("accT", [P, KD, NPAD])
            gT = sb("gT", [8, NPAD])
            LG = sb("LG", [P, NT, 8])
            with ExitStack() as c2:
                sb, pb, sem = scope(c2)
                TB = sb("TB", [P, NT, WF])
                acc = sb("acc", [P, NT, WF])
                AD = sb("AD", [P, NT, 2 * HEADS])
                ln = sb("ln", [P, 2, 16])
                prep("gatf", True, X, a["L2_ffn_W_gat"], 16, TB, XT=XT, attS=a["L2_ffn_att_src"].rearrange("h c -> (h c)"),
                     attD=a["L2_ffn_att_dst"].rearrange("h c -> (h c)"), AD=AD, table=tabf, c=4)
                edge_sum("gatf", LF, tabf, WF, acc, AD=AD, c=4)
                sent = []
                attention_end(TB, AD, acc, 4, a["L2_ffn_b_gat"], lambda step, t, v: step(nc.vector.tensor_copy(TB[:, t, 0:16], v)))
                bias_load(ln[:, 0, :], a["L2_ffn_ln_gamma"])
                bias_load(ln[:, 1, :], a["L2_ffn_ln_beta"])
                with ExitStack() as c3:
                    sb, _, sem = scope(c3)
                    mean, var, sq = sb("mean", [P, NT, 1]), sb("var", [P, NT, 1]), sb("sq", [P, NT, 16])
                    chain, var_ready, rooted = sem("chain"), sem("var_ready"), sem("rooted")
                    with nc.Block() as block:
                        @block.vector
                        def _(dve):
                            link = linker(dve, chain)
                            s16 = TB[:, :, 0:16]
                            full = [P, NT, 16]
                            link(nc.vector.tensor_reduce(mean[:, :, :], s16, AX, ALU.add))
                            link(nc.vector.tensor_scalar(mean[:, :, :], mean[:, :, :], 1 / 16, None, ALU.mult))
                            link(nc.vector.tensor_tensor(s16, s16, mean[:, :, :].to_broadcast(full), ALU.subtract))
                            link(nc.vector.tensor_tensor(sq[:, :, :], s16, s16, ALU.mult))
                            link(nc.vector.tensor_reduce(var[:, :, :], sq[:, :, :], AX, ALU.add))
                            nc.vector.engine_nop().then_inc(var_ready, 1)
                            dve.wait_ge(rooted, 1)
                            link(nc.vector.reciprocal(var[:, :, :], var[:, :, :]))
                            link(nc.vector.tensor_tensor(s16, s16, var[:, :, :].to_broadcast(full), ALU.mult))
                            link(nc.vector.tensor_tensor(s16, s16, ln[:, 0:1, :].to_broadcast(full), ALU.mult))
                            link(nc.vector.tensor_tensor(s16, s16, ln[:, 1:2, :].to_broadcast(full), ALU.add))
                            link(nc.vector.tensor_reduce(LG[:, :, 0:4], s16.rearrange("p t (h c) -> p t c h", c=4), AX, ALU.add))
                            link(nc.vector.tensor_scalar(LG[:, :, 0:4], LG[:, :, 0:4], 1 / HEADS, None, ALU.mult))

                        @block.scalar
                        def _(act):
                            act.wait_ge(var_ready, 1)
                            nc.scalar.activation(var[:, :, :], var[:, :, :], ACT.Sqrt, bias=eps[:, 0:1], scale=1 / 16).then_inc(rooted, 1)
            gates(LG, gT, 4)
            experts("ffn2", XT, gT, accT, 4, 512, ACT.Gelu, a["L2_ffn_W1"], a["L2_ffn_b1"], a["L2_ffn_W2"], a["L2_ffn_b2"])
            experts_end(accT)

        with ExitStack() as ctx:
            sb, pb, sem = scope(ctx)
            raw = sb("raw", [P, NT, W1TAB])
            TR = sb("TR", [P, NT, D])
            acc = sb("acc", [P, NT, W1TAB])
            bb = sb("bb", [P, D])
            rdeg = sb("rdeg", [P, NT])

            def mean_in(link, t):
                link(nc.vector.tensor_scalar(rdeg[:, t], acc[:, t, D], 1.0, None, ALU.max))
                link(nc.vector.reciprocal(rdeg[:, t], rdeg[:, t]))
                link(nc.vector.tensor_tensor(acc[:, t, 0:D], acc[:, t, 0:D], rdeg[:, t].unsqueeze(2).to_broadcast([P, TG, D]), ALU.mult))

            def hidden3(link, t):
                av = acc[:, t, 0:D]
                link(nc.vector.tensor_tensor(av, av, TR[:, t, :], ALU.add))
                link(nc.vector.tensor_tensor(av, av, tiles_bc(bb[:, :], D), ALU.add))
                link(nc.vector.tensor_scalar(av, av, 0.0, None, ALU.max))
            for n in (1, 2):
                prep(f"sage_r{n}", n == 1, X if n == 1 else acc, a[f"L3_gnn_W{n}_r"], D, TR, raw=raw, ones_col=D, table=tab1[n])
                edge_sum(f"sage{n}", LB, tab1[n], W1TAB, acc)
                sweep(3, mean_in)
                prep(f"sage_l{n}", False, acc, a[f"L3_gnn_W{n}_l"], D, acc)
                bias_load(bb[:, :], a[f"L3_gnn_b{n}"])
                if n == 1:
                    sweep(3, hidden3)
                else:
                    add_to_x(bb, [acc, TR])

        expert_layer("ffn3", 8, 1024, ACT.Gelu, a["L3_ffn_Wg"].rearrange("(k p) e -> p k e", p=P), [a["L3_ffn_bg"]],
                     a["L3_ffn_W1"], a["L3_ffn_b1"], a["L3_ffn_W2"], a["L3_ffn_b2"], last=True)


def kernel(**inputs):
    import numpy as _np
    import concourse.bacc as _bacc
    from concourse.bass_utils import run_bass_kernel_spmd as _run

    nc = _bacc.Bacc("TRN2", target_bir_lowering=False, num_devices=1)
    arrays, args = {}, {}
    for name in inputs:
        v = _np.ascontiguousarray(inputs[name])
        arrays[f"in_{name}"] = v
        args[name] = nc.dram_tensor(f"in_{name}", v.shape, mybir.dt.from_np(v.dtype), kind="ExternalInput").ap()
    out = nc.dram_tensor("out_0", (N, D), F32, kind="ExternalOutput").ap()
    program(nc, args, out)
    r = _run(nc, [arrays], core_ids=[0])
    return r.results[0]["out_0"]
```
